# Optimizing a Trainium2 kernel written in Bass

```python
import numpy as np
import jax
import jax.numpy as jnp

def _softmax(x, axis=-1):
    return jax.nn.softmax(x, axis=axis)

def _gelu(x):
    return jax.nn.gelu(x, approximate=True)

def _silu(x):
    return jax.nn.silu(x)

def _sigmoid(x):
    return jax.nn.sigmoid(x)

def _layernorm(x, axis=-1, eps=1e-05):
    m = jnp.mean(x, axis=axis, keepdims=True)
    v = jnp.var(x, axis=axis, keepdims=True)
    return (x - m) / jnp.sqrt(v + eps)

def _scatter_add(tgt, idx, src, axis=0):
    return tgt.at[idx].add(src)

def _segment_sum(src, seg, n):
    return jax.ops.segment_sum(src, seg, n)
kernel_name = 'mk_flamingo_gated_d1_seqx_r8_e7659c'

def setup_inputs(seed: int=0):
    np.random.seed(seed)
    _w = jnp.asarray

    def _rec_inputs():
        import jax
        import jax.numpy as jnp
        _rk = jax.random.key(seed)
        x = -0.0002928 + 1 * jax.random.normal(jax.random.fold_in(_rk, 1), (8, 256, 128), jnp.float32)
        _lenS = 256 - jax.random.randint(jax.random.fold_in(_rk, 7), (8,), 0, max(1, 256 // 4) + 1, jnp.int32)
        _lenS2 = 1601 - jax.random.randint(jax.random.fold_in(_rk, 8), (8,), 0, max(1, 1601 // 4) + 1, jnp.int32)
        _ctx_1024P = jax.random.normal(jax.random.fold_in(_rk, 11), (8, 16, 128), jnp.float32)
        _ctx_1024c = jax.random.dirichlet(jax.random.fold_in(_rk, 511), 0.3 * jnp.ones((16,), jnp.float32), (8, 1601))
        _ctx_1024t = jnp.einsum('bsk,bkd->bsd', _ctx_1024c, _ctx_1024P)
        _ctx_1024t = _ctx_1024t * jax.lax.rsqrt(jnp.mean(jnp.square(_ctx_1024t)) + 1e-12) * 0.953939
        ctx_1024 = -1.39393e-06 + 0.999914 * (_ctx_1024t + 0.3 * jax.random.normal(jax.random.fold_in(_rk, 611), (8, 1601, 128), jnp.float32))
        _validS = jnp.arange(256)[None, :] < _lenS[:, None]
        _validS2 = jnp.arange(1601)[None, :] < _lenS2[:, None]
        _causal = jnp.tril(jnp.ones((256, 256), dtype=bool))
        mask_SxS2_fk0 = jnp.where(jnp.broadcast_to(_validS2[0:1, :], (256, 1601)), -1000000000.0, 0.0).astype(jnp.float32)
        _g = jax.random.normal(jax.random.fold_in(_rk, 9001), (2, 1), jnp.float32)
        _g = jnp.sign(_g) * jnp.maximum(jnp.abs(_g), 1.0) + (_g == 0) * 1.0
        g_xattn = _g[0]
        g_ffn = _g[1]
        return (x, ctx_1024, mask_SxS2_fk0, g_xattn, g_ffn)
    x, ctx_1024, mask_SxS2_fk0, g_xattn, g_ffn = _rec_inputs()

    def _L0_xattn_setup():
        import jax, jax.numpy as jnp
        import numpy as np
        import math
        D_MODEL = 128
        NHEAD = 16
        HEAD_DIM = D_MODEL // NHEAD
        B, S = (2, 256)

        def _split_heads(x):
            b, s, _ = x.shape
            return x.reshape(b, s, NHEAD, HEAD_DIM).transpose(0, 2, 1, 3)
        key = jax.random.key(seed)
        ks = jax.random.split(key, 12)
        s = 1.0 / math.sqrt(D_MODEL)
        inp = {'query': jax.random.normal(ks[0], (B, S, D_MODEL), jnp.float32), 'key': jax.random.normal(ks[1], (B, S, D_MODEL), jnp.float32), 'value': jax.random.normal(ks[2], (B, S, D_MODEL), jnp.float32), 'attn_mask': jnp.where(jnp.tril(jnp.ones((S, S), bool)), 0.0, -jnp.inf).astype(jnp.float32), 'Wq': jax.random.normal(ks[3], (D_MODEL, D_MODEL), jnp.float32) * s, 'bq': jnp.zeros((D_MODEL,), jnp.float32), 'Wk': jax.random.normal(ks[4], (D_MODEL, D_MODEL), jnp.float32) * s, 'bk': jnp.zeros((D_MODEL,), jnp.float32), 'Wv': jax.random.normal(ks[5], (D_MODEL, D_MODEL), jnp.float32) * s, 'bv': jnp.zeros((D_MODEL,), jnp.float32), 'Wo': jax.random.normal(ks[6], (D_MODEL, D_MODEL), jnp.float32) * s, 'bo': jnp.zeros((D_MODEL,), jnp.float32)}
        return inp
    _L0_xattn_all = _L0_xattn_setup()
    _L0_xattn_in = {k: v for k, v in _L0_xattn_all.items() if k in ('Wq', 'bq', 'Wk', 'bk', 'Wv', 'bv', 'Wo', 'bo')}
    del _L0_xattn_all

    def _L0_ffn_setup():
        import jax, jax.numpy as jnp
        import numpy as np
        BITS = 8
        LORA_RANK = 16
        LORA_ALPHA = 32
        SCALING = LORA_ALPHA / LORA_RANK

        def fake_quant_weight(w, bits=BITS):
            qmax = 2.0 ** (bits - 1) - 1
            scale = jnp.max(jnp.abs(w)) / qmax
            wq = jnp.clip(jnp.round(w / scale), -qmax - 1, qmax) * scale
            return w + jax.lax.stop_gradient(wq - w)

        def qat_lora_linear(x, W, b, A, B):
            Wq = fake_quant_weight(W)
            base = jnp.einsum('bsi,oi->bso', x, Wq) + b
            lora = jnp.einsum('bsr,or->bso', jnp.einsum('bsi,ri->bsr', x, A), B)
            return base + SCALING * lora
        key = jax.random.key(seed)
        ks = jax.random.split(key, 9)
        d, f = (128, 512)
        s_in = 1.0 / np.sqrt(d)
        s_ff = 1.0 / np.sqrt(f)
        return {'hidden_states': jax.random.normal(ks[0], (4, 256, d), jnp.float32), 'W_fc': jax.random.normal(ks[1], (f, d), jnp.float32) * s_in, 'b_fc': jnp.zeros((f,), jnp.float32), 'A_fc': jax.random.normal(ks[2], (LORA_RANK, d), jnp.float32) * s_in, 'B_fc': jnp.zeros((f, LORA_RANK), jnp.float32), 'W_proj': jax.random.normal(ks[3], (d, f), jnp.float32) * s_ff, 'b_proj': jnp.zeros((d,), jnp.float32), 'A_proj': jax.random.normal(ks[4], (LORA_RANK, f), jnp.float32) * s_ff, 'B_proj': jnp.zeros((d, LORA_RANK), jnp.float32)}
    _L0_ffn_all = _L0_ffn_setup()
    _L0_ffn_in = {k: v for k, v in _L0_ffn_all.items() if k in ('W_fc', 'b_fc', 'A_fc', 'B_fc', 'W_proj', 'b_proj', 'A_proj', 'B_proj')}
    del _L0_ffn_all
    return {'x': x, 'ctx_1024': ctx_1024, 'mask_SxS2_fk0': mask_SxS2_fk0, 'g_xattn': g_xattn, 'g_ffn': g_ffn, 'L0_xattn_Wq': _L0_xattn_in['Wq'], 'L0_xattn_bq': _L0_xattn_in['bq'], 'L0_xattn_Wk': _L0_xattn_in['Wk'], 'L0_xattn_bk': _L0_xattn_in['bk'], 'L0_xattn_Wv': _L0_xattn_in['Wv'], 'L0_xattn_bv': _L0_xattn_in['bv'], 'L0_xattn_Wo': _L0_xattn_in['Wo'], 'L0_xattn_bo': _L0_xattn_in['bo'], 'L0_ffn_W_fc': _L0_ffn_in['W_fc'], 'L0_ffn_b_fc': _L0_ffn_in['b_fc'], 'L0_ffn_A_fc': _L0_ffn_in['A_fc'], 'L0_ffn_B_fc': _L0_ffn_in['B_fc'], 'L0_ffn_W_proj': _L0_ffn_in['W_proj'], 'L0_ffn_b_proj': _L0_ffn_in['b_proj'], 'L0_ffn_A_proj': _L0_ffn_in['A_proj'], 'L0_ffn_B_proj': _L0_ffn_in['B_proj']}

def reference(x, ctx_1024, mask_SxS2_fk0, g_xattn, g_ffn, L0_xattn_Wq, L0_xattn_bq, L0_xattn_Wk, L0_xattn_bk, L0_xattn_Wv, L0_xattn_bv, L0_xattn_Wo, L0_xattn_bo, L0_ffn_W_fc, L0_ffn_b_fc, L0_ffn_A_fc, L0_ffn_B_fc, L0_ffn_W_proj, L0_ffn_b_proj, L0_ffn_A_proj, L0_ffn_B_proj):
    import jax
    import jax.numpy as jnp

    def _L0_xattn_ref(query, key, value, attn_mask, Wq, bq, Wk, bk, Wv, bv, Wo, bo):
        import jax, jax.numpy as jnp
        import numpy as np
        import math
        D_MODEL = 128
        NHEAD = 16
        HEAD_DIM = D_MODEL // NHEAD
        B, S = (2, 256)

        def _split_heads(x):
            b, s, _ = x.shape
            return x.reshape(b, s, NHEAD, HEAD_DIM).transpose(0, 2, 1, 3)
        q = _split_heads(query @ Wq + bq)
        k = _split_heads(key @ Wk + bk)
        v = _split_heads(value @ Wv + bv)
        scores = jnp.einsum('bhqd,bhkd->bhqk', q, k) / math.sqrt(HEAD_DIM)
        scores = scores + attn_mask[None, None, :, :]
        scores = jnp.where(jnp.isnan(scores), 0.0, scores)
        all_inf = jnp.all(jnp.isinf(scores), axis=-1, keepdims=True)
        scores = jnp.where(all_inf, 0.0, scores)
        attn = jax.nn.softmax(scores, axis=-1)
        attn = jnp.where(jnp.isnan(attn), 0.0, attn)
        ctx = jnp.einsum('bhqk,bhkd->bhqd', attn, v)
        ctx = ctx.transpose(0, 2, 1, 3).reshape(query.shape[0], query.shape[1], D_MODEL)
        return ctx @ Wo + bo

    def _L0_ffn_ref(hidden_states, W_fc, b_fc, A_fc, B_fc, W_proj, b_proj, A_proj, B_proj):
        import jax, jax.numpy as jnp
        import numpy as np
        BITS = 8
        LORA_RANK = 16
        LORA_ALPHA = 32
        SCALING = LORA_ALPHA / LORA_RANK

        def fake_quant_weight(w, bits=BITS):
            qmax = 2.0 ** (bits - 1) - 1
            scale = jnp.max(jnp.abs(w)) / qmax
            wq = jnp.clip(jnp.round(w / scale), -qmax - 1, qmax) * scale
            return w + jax.lax.stop_gradient(wq - w)

        def qat_lora_linear(x, W, b, A, B):
            Wq = fake_quant_weight(W)
            base = jnp.einsum('bsi,oi->bso', x, Wq) + b
            lora = jnp.einsum('bsr,or->bso', jnp.einsum('bsi,ri->bsr', x, A), B)
            return base + SCALING * lora
        h = qat_lora_linear(hidden_states, W_fc, b_fc, A_fc, B_fc)
        h = jax.nn.gelu(h, approximate=False)
        h = qat_lora_linear(h, W_proj, b_proj, A_proj, B_proj)
        return h
    x = x + jnp.tanh(g_xattn[0]) * _L0_xattn_ref(_layernorm(x, axis=-1), ctx_1024, ctx_1024, mask_SxS2_fk0, L0_xattn_Wq, L0_xattn_bq, L0_xattn_Wk, L0_xattn_bk, L0_xattn_Wv, L0_xattn_bv, L0_xattn_Wo, L0_xattn_bo)
    x = x + jnp.tanh(g_ffn[0]) * _L0_ffn_ref(_layernorm(x, axis=-1), L0_ffn_W_fc, L0_ffn_b_fc, L0_ffn_A_fc, L0_ffn_B_fc, L0_ffn_W_proj, L0_ffn_b_proj, L0_ffn_A_proj, L0_ffn_B_proj)
    return x

_drawn_inputs = setup_inputs


def setup_inputs(seed=0):
    import zlib

    import numpy as np

    out = dict(_drawn_inputs(seed))
    spreads = {'L0_xattn_bq': (0.0, 0.436),
     'L0_xattn_bk': (0.0, 0.8),
     'L0_xattn_bv': (0.0, 0.1),
     'L0_xattn_bo': (0.0, 0.1),
     'L0_ffn_b_fc': (0.0, 0.1),
     'L0_ffn_B_fc': (0.0, 0.1),
     'L0_ffn_b_proj': (0.0, 0.1),
     'L0_ffn_B_proj': (0.0, 0.1)}
    factors = {}
    for name, (base, spread) in spreads.items():
        noise = np.random.default_rng([zlib.crc32(name.encode()), seed]).standard_normal(out[name].shape)
        drawn = base * np.exp(spread * noise) if base else spread * noise
        out[name] = jnp.asarray(drawn.astype(out[name].dtype))
    for name, factor in factors.items():
        out[name] = (out[name] * factor).astype(out[name].dtype)
    return out
```

```python
import concourse.bass as bass
from concourse import mybir
from contextlib import ExitStack


def flamingo_block(nc, io):
    fp32, bf16, i32 = mybir.dt.float32, mybir.dt.bfloat16, mybir.dt.int32
    ALU = mybir.AluOpType
    ACT = mybir.ActivationFunctionType
    AX = mybir.AxisListType

    B, S, D = io["x"].shape
    KEYS = io["ctx_1024"].shape[1]
    F = io["L0_ffn_W_fc"].shape[0]
    RANK = io["L0_ffn_A_fc"].shape[0]
    P = 128
    NH, HD = 16, D // 16
    HG = 4
    G = NH // HG
    QT = S // P
    KT = -(-KEYS // P)
    TAIL = KEYS - (KT - 1) * P
    BANK = 512
    HALF = (KEYS + 1) // 2
    PARTS = 3
    K_PART = [0, 1, 2, 0, 1, 0]
    Q_PART = [0, 0, 0, 1, 1, 2]
    TERMS = len(K_PART)
    TR = TERMS * HD
    XR = 2 * PARTS
    KR = XR + TR
    FC = F // P
    TOK = B * S
    QSCALE = float(HD) ** -0.5
    BIG = 3.0e38
    PLAIN_TOP = 1024.0
    EPS = 1e-5
    QMAX = 127.0
    MAGIC = 1.5 * 2.0 ** 23
    CHUNKS = 2 * QT * HG
    LEAD = 5
    MX_STEP = 10

    def key_rows(t):
        return P if t < KT - 1 else TAIL

    def settled(eng, sem_, value):
        eng.wait_ge(sem_, value)
        eng.sem_inc(passed, 1)

    def cuts(width):
        return [(a, min(a + BANK, width)) for a in range(0, width, BANK)]

    with ExitStack() as ctx:
        def sb(name, shape, dt):
            return ctx.enter_context(nc.sbuf_tensor(name, shape, dt))

        def sem(name):
            return ctx.enter_context(nc.semaphore(name))

        ps = ctx.enter_context(nc.psum_tensor("ps", [P, 8, BANK], fp32))

        def bank(n):
            return ps[:, n, :]

        k_op = sb("k_op", [P, G * HG * KEYS], bf16)
        q1_op = sb("q1_op", [KR, G, HG, S], bf16)
        q2_op = sb("q2_op", [KR, G, HG * S], bf16)
        v_in = sb("v_in", [P, KT, D], fp32)
        v_op = sb("v_op", [P, G, KT, HG, 32], fp32)
        mask_q = sb("mask_q", [P, QT, KEYS], fp32)
        maskT = sb("maskT", [P, KT, PARTS, S], bf16)
        x_sb = sb("x_sb", [P, B * QT, D], fp32)
        ot = sb("ot", [P, B * G, S], fp32)
        pt = sb("pt", [P, 4, HG * S], fp32)
        junk = sb("junk", [P, HALF], fp32)
        w_qkv = sb("w_qkv", [P, 3, D], fp32)
        b_qk = sb("b_qk", [P, 3], fp32)
        bv_all = sb("bv_all", [P, D], fp32)
        w_o = sb("w_o", [P, G, D], fp32)
        sel = sb("sel", [P, P], fp32)
        ident = sb("ident", [P, P], fp32)
        identb = sb("identb", [P, P], bf16)
        ones_m = sb("ones_m", [KR, P], bf16)
        ones_f = sb("ones_f", [PARTS, P], fp32)
        ext = sb("ext", [XR, KEYS], bf16)
        gates = sb("gates", [P, 2], fp32)
        tgates = sb("tgates", [P, 2], fp32)
        stat = sb("stat", [P, PARTS], fp32)
        rng = sb("rng", [P, 4], fp32)
        stat_t = sb("stat_t", [PARTS, 1], fp32)
        stat_d = sb("stat_d", [PARTS, PARTS], fp32)
        allstat = sb("allstat", [P, PARTS], fp32)
        plain = sb("plain", [P, 1], fp32)
        general_i = sb("general_i", [1, 1], i32)
        half_neg = sb("half_neg", [P, B * QT], fp32)
        ln_sum = sb("ln_sum", [P, B * QT], fp32)
        ln_mean = sb("ln_mean", [P, B * QT], fp32)
        ln_var = sb("ln_var", [P, B * QT], fp32)
        ln_rstd = sb("ln_rstd", [P, B * QT], fp32)
        mx_part = sb("mx_part", [P, 2, HG * QT, 2], fp32)
        mx_neg = sb("mx_neg", [P, 2, HG * QT], fp32)
        mx_res = sb("mx_res", [P, 2, HG * QT], fp32)
        mx_bf = sb("mx_bf", [P, 2, HG * QT, PARTS], bf16)
        w_fcT = sb("w_fcT", [P, F], fp32)
        w_pjT = sb("w_pjT", [P, FC, D], fp32)
        b_fc = sb("b_fc", [P, FC], fp32)
        b_pj = sb("b_pj", [P, D], fp32)
        l_sum = sb("l_sum", [P, 2, QT], fp32)
        l_rstd = sb("l_rstd", [P, 2, QT], fp32)

        kv_k = k_op[:, :].rearrange("p (g h k) -> p g h k", g=G, h=HG)
        k_pool = k_op[:, 0:2 * PARTS * KEYS].rearrange("p (b a k) -> p b a k", b=2, a=PARTS)
        off = 2 * PARTS * KEYS + (2 * PARTS * KEYS) % 2
        v_out = k_op[:, off:off + 4 * KT * D].bitcast(fp32).rearrange("p (b t d) -> p b t d", b=2, t=KT)
        k_res = k_op[:, off + 4 * KT * D:off + 4 * KT * D + 2 * KEYS].bitcast(fp32)
        ot_flat = ot[:, :, :].rearrange("p u s -> p (u s)")
        ctx_in = ot_flat[:, 0:2 * KT * D].rearrange("p (b t d) -> p b t d", b=2, t=KT)
        ctxT = ot_flat[:, 2 * KT * D:2 * KT * D + 2 * KEYS].rearrange("p (b k) -> p b k", b=2)
        pt_flat = pt[:, :, :].rearrange("p n s -> p (n s)")
        k_full = pt_flat[:, 0:2 * KEYS].rearrange("p (b k) -> p b k", b=2)
        qn = ot_flat[:, 0:TOK].rearrange("p (t d) -> p t d", d=D)
        qc = ot_flat[:, TOK:2 * TOK].rearrange("p (t d) -> p t d", d=D)
        qsq = ot_flat[:, 2 * TOK:3 * TOK].rearrange("p (t d) -> p t d", d=D)
        xnT = ot_flat[:, 3 * TOK:4 * TOK]
        q_full = pt_flat[:, 0:TOK]
        q_res = pt_flat[:, TOK:2 * TOK]
        q_bf = k_op[:, 0:PARTS * TOK].rearrange("p (a s) -> p a s", a=PARTS)
        m_off = PARTS * TOK
        mT_full = k_op[:, m_off:m_off + 2 * KT * S].bitcast(fp32)
        mT_res = k_op[:, m_off + 2 * KT * S:m_off + 4 * KT * S].bitcast(fp32)
        mask0 = v_in[:, :, :].rearrange("p t d -> p (t d)")[:, 0:KEYS]
        m0_off = m_off + 4 * KT * S
        m0_hi = k_op[:, m0_off:m0_off + PARTS * KEYS]
        m0_res = q_res[:, 0:KEYS]
        extf = junk[:, :].bitcast(bf16)[0:XR, 0:KEYS]
        wf_in = v_op[:, 0, 0:4, :, :].rearrange("p t h c -> p (t h c)")
        wp_in = v_op[:, 1, 0:4, :, :].rearrange("p t h c -> p (t h c)")
        wf_a = v_op[:, 2, 0:4, :, :].rearrange("p t h c -> p (t h c)")
        wf_b = v_op[:, 3, 0:4, :, :].rearrange("p t h c -> p (t h c)")
        wf_r = v_in[:, 0:4, :].rearrange("p t d -> p (t d)")
        wp_r = v_in[:, 4:8, :].rearrange("p t d -> p (t d)")
        inv_s = sb("inv_s", [P, 4], fp32)
        a_fc = sb("a_fc", [RANK, D], fp32)
        bl_fc = sb("bl_fc", [P, FC, RANK], fp32)
        a_pj = v_op[0:RANK, 0, 4:8, :, :].rearrange("p t h c -> p (t h c)")
        bl_pj = sb("bl_pj", [P, RANK], fp32)
        blT_fc = v_op[0:RANK, 1, 4:8, :, :].rearrange("p t h c -> p (t h c)")
        blT_pj = sb("blT_pj", [RANK, D], fp32)
        v_flat = v_op[:, :, :, :, :].rearrange("p g t h c -> p (g t h c)")
        x_mid, x_res, x_c, x_n, out_sb = [
            v_flat[:, k * 2 * QT * D:(k + 1) * 2 * QT * D].rearrange("p (b t d) -> p b t d", b=2, t=QT) for k in range(5)]
        x_nT = v_flat[:, 10 * QT * D:12 * QT * D].rearrange("p (b s) -> p b s", b=2)
        otn = pt_flat[:, 0:2 * G * S].rearrange("p (b g s) -> p b g s", b=2, g=G)
        hT = pt_flat[:, 2 * G * S:2 * G * S + 2 * FC * S].rearrange("p (b c s) -> p b c s", b=2, c=FC)

        k_scr = nc.dram_tensor("k_scr", [B, NH, PARTS, HD, KEYS], bf16, kind="Internal").ap()
        q_scr = nc.dram_tensor("q_scr", [NH, TERMS, HD, B * S], bf16, kind="Internal").ap()
        v_scr = nc.dram_tensor("v_scr", [B, KT, P, D], fp32, kind="Internal").ap()

        passed = sem("passed")
        x_loaded = sem("x_loaded")
        proj_loaded = sem("proj_loaded")
        mask_loaded = sem("mask_loaded")
        ffn_loaded = sem("ffn_loaded")
        wo_loaded = sem("wo_loaded")
        consts = sem("consts")
        pool_chain = sem("pool_chain")
        dve_chain = sem("dve_chain")
        act_chain = sem("act_chain")
        ln_ready = sem("ln_ready")
        rstd_ready = sem("rstd_ready")
        xn_ready = sem("xn_ready")
        xnT_ps = sem("xnT_ps")
        xnT_sb = sem("xnT_sb")
        q_ps = sem("q_ps")
        q_ev = sem("q_ev")
        q_split = sem("q_split")
        q_stored = sem("q_stored")
        clamp = sem("clamp")
        mT_ps = sem("mT_ps")
        mT_sb = sem("mT_sb")
        mT_split = sem("mT_split")
        m0_split = sem("m0_split")
        ext_in = sem("ext_in")
        ext_flag = sem("ext_flag")
        ext_out = sem("ext_out")
        stat_ready = sem("stat_ready")
        stat_ps = sem("stat_ps")
        stat_diag = sem("stat_diag")
        stat_bc = sem("stat_bc")
        flag_ready = sem("flag_ready")
        wq_ready = sem("wq_ready")
        lora_ps = sem("lora_ps")
        lora_sb = sem("lora_sb")
        weff_ps = sem("weff_ps")
        weff_sb = sem("weff_sb")
        v_op_set = sem("v_op_set")
        ctx_loaded = [sem(f"ctx_loaded{p}") for p in range(2)]
        kv_stored = [sem(f"kv_stored{p}") for p in range(2)]
        ctxT_ps = sem("ctxT_ps")
        ctxT_sb = sem("ctxT_sb")
        k_ps = sem("k_ps")
        k_ev = sem("k_ev")
        v_ps = sem("v_ps")
        v_ev = sem("v_ev")
        k_split = sem("k_split")
        kq_loaded = [sem(f"kq_loaded{g}") for g in range(G)]
        v_loaded = sem("v_loaded")
        v_op_ready = sem("v_op_ready")
        s1_ready = sem("s1_ready")
        s1_done = sem("s1_done")
        mx_ready = sem("mx_ready")
        mx_split = sem("mx_split")
        mxT_ps = sem("mxT_ps")
        mxT_sb = sem("mxT_sb")
        s2_ready = sem("s2_ready")
        exp_done = sem("exp_done")
        pv_done = sem("pv_done")
        o_done = sem("o_done")
        r_ps = sem("r_ps")
        r_inv = sem("r_inv")
        otn_sb = sem("otn_sb")
        y_ps = sem("y_ps")
        mid_ready = sem("mid_ready")
        mid_sum = sem("mid_sum")
        mid_rstd = sem("mid_rstd")
        xn2_ready = sem("xn2_ready")
        xT2_ps = sem("xT2_ps")
        xT2_sb = sem("xT2_sb")
        h_ps = sem("h_ps")
        h_sb = sem("h_sb")
        out_ps = sem("out_ps")
        out_ready = sem("out_ready")
        out_stored = [sem(f"out_stored{p}") for p in range(2)]

        block = ctx.enter_context(nc.Block())

        TT = (KT + 3) // 4
        CH = cuts(KEYS)

        def chunk_pos(step):
            return CHUNKS * step // KT

        @block.sync
        def _(sp):
            sp.dma_start(x_sb[:, :, :], io["x"].rearrange("b (t p) d -> p (b t) d", p=P)).then_inc(x_loaded, 16)
            for n, w in enumerate(("Wq", "Wk", "Wv")):
                sp.dma_start(w_qkv[:, n, :], io["L0_xattn_" + w]).then_inc(proj_loaded, 16)
            sp.dma_start(b_qk[:, 0:1], io["L0_xattn_bq"].rearrange("(d a) -> d a", a=1)).then_inc(proj_loaded, 16)
            sp.dma_start(b_qk[:, 1:2], io["L0_xattn_bk"].rearrange("(d a) -> d a", a=1)).then_inc(proj_loaded, 16)
            sp.dma_start(bv_all[:, :], io["L0_xattn_bv"].rearrange("(a d) -> a d", a=1).to_broadcast([P, D])).then_inc(proj_loaded, 16)
            sp.dma_start(mask_q[:, :, :], io["mask_SxS2_fk0"].rearrange("(t p) k -> p t k", p=P)).then_inc(mask_loaded, 16)
            sp.dma_start(mask0[:, :], io["mask_SxS2_fk0"][0:1, :].to_broadcast([P, KEYS])).then_inc(mask_loaded, 16)
            sp.wait_ge(wq_ready, 1)
            for j in range(HG):
                sp.dma_start(w_o[32 * j:32 * j + HD, :, :],
                             io["L0_xattn_Wo"].rearrange("(g j d) n -> j d g n", g=G, j=HG)[j]).then_inc(wo_loaded, 16)
            sp.dma_start(w_o[HD:HD + 1, 0, :], io["L0_xattn_bo"].rearrange("(a d) -> a d", a=1)).then_inc(wo_loaded, 16)

            sp.wait_ge(m0_split, 1)
            for a in range(PARTS):
                sp.dma_start(ext[PARTS + a:PARTS + a + 1, :], m0_hi[0:1, a * KEYS:(a + 1) * KEYS]).then_inc(ext_in, 16)
            sp.wait_ge(q_split, 3)
            for t in range(TERMS):
                sp.dma_start(q_scr[:, t, :, :].rearrange("h d s -> h d s"), q_bf[:, Q_PART[t], :]).then_inc(q_stored, 16)
            sp.wait_ge(q_stored, 16 * TERMS)
            sp.wait_ge(mT_split, 4)

            def load_ctx(b, p):
                full = (KT - 1) * P
                sp.dma_start(ctx_in[:, p, 0:KT - 1, :],
                             io["ctx_1024"][b, 0:full, :].rearrange("(t p) d -> p t d", p=P)).then_inc(ctx_loaded[p], 16)
                sp.dma_start(ctx_in[0:TAIL, p, KT - 1, :], io["ctx_1024"][b, full:KEYS, :]).then_inc(ctx_loaded[p], 16)

            def store_kv(b, p):
                for a in range(PARTS):
                    sp.dma_start(k_scr[b, :, a, :, :], k_pool[:, p, a, :]).then_inc(kv_stored[p], 16)
                sp.dma_start(v_scr[b, 0:KT - 1, :, :].rearrange("t p d -> p t d"), v_out[:, p, 0:KT - 1, :]).then_inc(kv_stored[p], 16)
                sp.dma_start(v_scr[b, KT - 1, 0:TAIL, :], v_out[0:TAIL, p, KT - 1, :]).then_inc(kv_stored[p], 16)

            sp.wait_ge(xnT_sb, 4)
            sp.wait_ge(q_ps, 4)
            load_ctx(0, 0)
            load_ctx(1, 1)
            with sp.Fori(0, B // 2) as i:
                for p in range(2):
                    sp.wait_ge(k_split, 2 * i + p + 1 + 2)
                    sp.wait_ge(v_ev, TT * (2 * i + p + 1) + 2)
                    store_kv(2 * i + p, p)
                    sp.wait_ge(ctxT_ps, TT * (2 * i + p + 1))
                    nxt = (2 * i + p + 2) % B
                    load_ctx(nxt, p)
            for p in range(2):
                sp.wait_ge(kv_stored[p], 80 * (B // 2 + 1))
                sp.wait_ge(ctx_loaded[p], 32 * (B // 2 + 1))
            sp.wait_ge(ext_flag, 1)
            for g in range(G):
                sp.dma_start(kv_k[0:XR, g, :, :], extf[:, :].unsqueeze(1).to_broadcast([XR, HG, KEYS])).then_inc(ext_out, 16)

            def load_unit(b, g):
                h0 = HG * g
                for r0, np_ in ((0, 3), (3, 2), (5, 1)):
                    sp.dma_start(kv_k[XR + HD * r0:XR + HD * (r0 + np_), g, :, :],
                                 k_scr[b, h0:h0 + HG, 0:np_, :, :].rearrange("h a d k -> (a d) h k")).then_inc(kq_loaded[g], 16)
                src = q_scr[h0:h0 + HG, :, :, bass.ds(b * S, S)].rearrange("h t d s -> (t d) h s")
                sp.dma_start(q1_op[XR:KR, g, :, :], src).then_inc(kq_loaded[g], 16)
                sp.dma_start(q2_op[XR:KR, g, :].rearrange("r (h s) -> r h s", h=HG), src).then_inc(kq_loaded[g], 16)

            def load_v(b):
                sp.dma_start(v_in[:, 0:KT - 1, :], v_scr[b, 0:KT - 1, :, :].rearrange("t p d -> p t d")).then_inc(v_loaded, 16)
                sp.dma_start(v_in[0:TAIL, KT - 1, :], v_scr[b, KT - 1, 0:TAIL, :]).then_inc(v_loaded, 16)

            load_v(0)
            for g in range(G):
                load_unit(0, g)
            with sp.Fori(1, B) as i:
                for g in range(G):
                    if g == 0:
                        sp.wait_ge(v_op_ready, G * i)
                        load_v(i)
                    sp.wait_ge(o_done, G * i + g + 1)
                    load_unit(i, g)

            def store_out(b, p):
                sp.dma_start(io["out"][b].rearrange("(t p) d -> p t d", p=P), out_sb[:, p, :, :]).then_inc(out_stored[p], 16)

            with sp.Fori(0, B // 2) as i:
                for p in range(2):
                    sp.wait_ge(out_ready, QT * (2 * i + p + 1))
                    store_out(2 * i + p, p)
            for p in range(2):
                sp.wait_ge(out_stored[p], 16 * (B // 2 + 1))

        @block.gpsimd
        def _(pool):
            n = [0]

            def link(ins):
                n[0] += 1
                ins.then_inc(pool_chain, 1)
                pool.wait_ge(pool_chain, n[0])

            nc.gpsimd.memset(half_neg[:, :], -0.5)
            link(nc.gpsimd.memset(ident[:, :], 0.0))
            link(nc.gpsimd.affine_select(out=ident[:, :], in_=ident[:, :], compare_op=ALU.not_equal, fill=1.0,
                                         base=0, pattern=[[-1, P]], channel_multiplier=1))
            nc.gpsimd.tensor_copy(identb[:, :], ident[:, :]).then_inc(consts, 1)
            link(nc.gpsimd.memset(sel[:, :], 0.0))
            nc.gpsimd.affine_select(out=sel[:, :].rearrange("p (j r) -> p j r", j=HG), in_=sel[:, :].rearrange("p (j r) -> p j r", j=HG),
                                    compare_op=ALU.not_equal, fill=1.0, base=-HD,
                                    pattern=[[-32, HG], [0, 32]], channel_multiplier=1).then_inc(consts, 1)
            link(nc.gpsimd.memset(ones_m[:, :], 0.0))
            nc.gpsimd.memset(ones_m[0:PARTS, :], 1.0).then_inc(consts, 1)
            nc.gpsimd.memset(ones_f[:, :], 1.0).then_inc(consts, 1)
            nc.gpsimd.memset(ext[:, :], 1.0).then_inc(consts, 1)
            nc.gpsimd.memset(q1_op[0:XR, :, :, :], 0.0).then_inc(consts, 1)
            nc.gpsimd.memset(q2_op[0:XR, :, :], 1.0).then_inc(consts, 1)
            pool.wait_ge(ln_ready, 1)
            link(nc.gpsimd.tensor_scalar(ln_var[:, :], ln_var[:, :], 1.0 / D, EPS, ALU.mult, ALU.add))
            nc.gpsimd.tensor_tensor(ln_rstd[:, :], ln_var[:, :], half_neg[:, :], ALU.pow).then_inc(rstd_ready, 1)
            for t0, t1 in ((0, KT - 1), (KT - 1, KT)):
                rows = P if t0 == 0 else TAIL
                full = mT_full[0:rows, t0 * S:t1 * S].rearrange("p (t s) -> p t s", s=S)
                res = mT_res[0:rows, t0 * S:t1 * S].rearrange("p (t s) -> p t s", s=S)
                if t0 == 0:
                    pool.wait_ge(mT_sb, KT)
                link(nc.gpsimd.tensor_copy(maskT[0:rows, t0:t1, 0, :], full))
                link(nc.gpsimd.tensor_tensor(res, full, maskT[0:rows, t0:t1, 0, :], ALU.subtract))
                nc.gpsimd.tensor_copy(maskT[0:rows, t0:t1, 1, :], res).then_inc(mT_split, 1)
                pool.wait_ge(mT_split, 1 if t0 == 0 else 3)
                nc.gpsimd.tensor_tensor(maskT[0:rows, t0:t1, 2, :], res, maskT[0:rows, t0:t1, 1, :], ALU.subtract).then_inc(mT_split, 1)
            pool.wait_ge(weff_sb, 2)
            link(nc.gpsimd.memset(v_op[:, :, :, :, :], 0.0))
            nc.gpsimd.memset(v_op[:, :, :, :, HD:HD + 1], 1.0).then_inc(v_op_set, 1)
            pool.wait_ge(v_op_set, 1)

            def spread_v(b, g):
                src = v_in[:, :, HD * HG * g:HD * HG * (g + 1)].rearrange("p t (h d) -> p t h d", h=HG)
                nc.gpsimd.tensor_copy(v_op[:, g, 0:KT - 1, :, 0:HD], src[:, 0:KT - 1])
                nc.gpsimd.tensor_copy(v_op[0:TAIL, g, KT - 1, :, 0:HD], src[0:TAIL, KT - 1]).then_inc(v_op_ready, 1)

            def split_max(u, par):
                settled(pool, mx_ready, u + 1)
                nc.gpsimd.tensor_copy(mx_bf[:, par, :, 0], mx_neg[:, par, :]).then_inc(mx_split, 1)
                pool.wait_ge(mx_split, 4 * u + 1)
                nc.gpsimd.tensor_tensor(mx_res[:, par, :], mx_neg[:, par, :], mx_bf[:, par, :, 0], ALU.subtract).then_inc(mx_split, 1)
                settled(pool, mx_split, 4 * u + 2)
                nc.gpsimd.tensor_copy(mx_bf[:, par, :, 1], mx_res[:, par, :]).then_inc(mx_split, 1)
                pool.wait_ge(mx_split, 4 * u + 3)
                nc.gpsimd.tensor_tensor(mx_bf[:, par, :, 2], mx_res[:, par, :], mx_bf[:, par, :, 1], ALU.subtract).then_inc(mx_split, 1)

            def unit(i, g, last):
                if last and g == G - 1:
                    return
                nxt = G * i + g + 1
                split_max(nxt, (g + 1) % 2)
                if g == G - 1:
                    pool.wait_ge(v_loaded, 32 * (i + 2))
                settled(pool, o_done, nxt + 1)
                spread_v(i + (g + 1) // G, (g + 1) % G)

            split_max(0, 0)
            pool.wait_ge(v_loaded, 32)
            spread_v(0, 0)
            with pool.Fori(0, B - 1) as i:
                for g in range(G):
                    unit(i, g, False)
            for g in range(G):
                unit(B - 1, g, True)

            def rstd(b, p):
                settled(pool, mid_sum, b + 1)
                nc.gpsimd.tensor_scalar(l_sum[:, p, :], l_sum[:, p, :], 1.0 / D, EPS, ALU.mult, ALU.add).then_inc(mid_rstd, 1)
                pool.wait_ge(mid_rstd, 2 * b + 1)
                nc.gpsimd.tensor_tensor(l_rstd[:, p, :], l_sum[:, p, :], half_neg[:, 0:QT], ALU.pow).then_inc(mid_rstd, 1)

            with pool.Fori(0, B // 2) as i:
                for p in range(2):
                    rstd(2 * i + p, p)

        @block.scalar
        def _(act):
            act.dma_start(wf_in.rearrange("p (c d) -> p c d", c=FC), io["L0_ffn_W_fc"].rearrange("(c p) d -> p c d", p=P)).then_inc(ffn_loaded, 16)
            act.dma_start(wp_in, io["L0_ffn_W_proj"]).then_inc(ffn_loaded, 16)
            act.dma_start(gates[:, 0:1], io["g_xattn"].rearrange("(a d) -> a d", a=1).to_broadcast([P, 1])).then_inc(ffn_loaded, 16)
            act.dma_start(gates[:, 1:2], io["g_ffn"].rearrange("(a d) -> a d", a=1).to_broadcast([P, 1])).then_inc(ffn_loaded, 16)
            act.dma_start(a_fc[:, :], io["L0_ffn_A_fc"]).then_inc(ffn_loaded, 16)
            act.dma_start(bl_fc[:, :, :], io["L0_ffn_B_fc"].rearrange("(c p) r -> p c r", p=P)).then_inc(ffn_loaded, 16)
            act.dma_start(a_pj, io["L0_ffn_A_proj"]).then_inc(ffn_loaded, 16)
            act.dma_start(bl_pj[:, :], io["L0_ffn_B_proj"]).then_inc(ffn_loaded, 16)
            act.dma_start(b_fc[:, :], io["L0_ffn_b_fc"].rearrange("(c p) -> p c", p=P),
                          allow_slow_non_contiguous=True).then_inc(ffn_loaded, 16)
            act.dma_start(b_pj[:, :], io["L0_ffn_b_proj"].rearrange("(a d) -> a d", a=1).to_broadcast([P, D])).then_inc(ffn_loaded, 16)
            act.wait_ge(ffn_loaded, 160)
            act.activation(tgates[:, :], gates[:, :], ACT.Tanh).then_inc(act_chain, 1)
            act.wait_ge(lora_ps, 1)
            nc.scalar.mul(blT_fc, bank(7)[0:RANK, :], 2.0).then_inc(lora_sb, 1)
            act.wait_ge(lora_ps, 2)
            nc.scalar.mul(blT_pj[:, :], bank(6)[0:RANK, 0:D], 2.0).then_inc(lora_sb, 1)
            for c in range(4):
                act.wait_ge(xnT_ps, c + 1)
                act.activation(xnT[:, c * BANK:(c + 1) * BANK], bank(c), ACT.Copy).then_inc(xnT_sb, 1)
            act.wait_ge(proj_loaded, 96)
            nc.scalar.mul(b_qk[:, 2:3], b_qk[:, 0:1], QSCALE).then_inc(act_chain, 1)
            act.wait_ge(act_chain, 2)
            for c in range(4):
                act.wait_ge(q_ps, c + 1)
                cs = slice(c * BANK, (c + 1) * BANK)
                act.activation(q_full[:, cs], bank(c), ACT.Identity, bias=b_qk[:, 2:3], scale=QSCALE)
                act.activation(q_bf[:, 0, cs], bank(c), ACT.Identity, bias=b_qk[:, 2:3], scale=QSCALE).then_inc(q_ev, 1)
            for t in range(KT):
                r = key_rows(t)
                act.wait_ge(mT_ps, t + 1)
                act.activation(mT_full[0:r, t * S:(t + 1) * S], bank(4 + t % 2)[0:r, 0:S], ACT.Copy).then_inc(mT_sb, 1)
            act.wait_ge(weff_ps, 1)
            act.activation(w_fcT[:, :], bank(6), ACT.Copy).then_inc(weff_sb, 1)
            act.wait_ge(weff_ps, 2)
            act.activation(w_pjT[:, :, :].rearrange("p c d -> p (c d)"), bank(7), ACT.Copy).then_inc(weff_sb, 1)

            act.wait_ge(q_split, 3)
            act.wait_ge(q_stored, 16 * TERMS)
            act.wait_ge(mT_split, 4)
            with act.Fori(0, B // 2) as i:
                for p in range(2):
                    b = 2 * i + p

                    def take_ctx(c):
                        m = TT * b + c
                        lo, hi = CH[c]
                        act.wait_ge(v_ps, m + 1)
                        act.wait_ge(ctxT_ps, m + 1)
                        act.activation(ctxT[:, p, lo:hi], bank(c % 2)[:, 0:hi - lo], ACT.Copy).then_inc(ctxT_sb, 1)

                    def take_k(c):
                        m = TT * b + c
                        lo, hi = CH[c]
                        act.wait_ge(k_ps, m + 1)
                        act.activation(k_full[:, p, lo:hi], bank(2 + c % 2)[:, 0:hi - lo], ACT.Identity, bias=b_qk[:, 1:2])
                        act.activation(k_pool[:, p, 0, lo:hi], bank(2 + c % 2)[:, 0:hi - lo], ACT.Identity, bias=b_qk[:, 1:2]).then_inc(k_ev, 1)

                    act.wait_ge(k_split, b + 1)
                    act.wait_ge(kv_stored[p], 80 * (i + 1))
                    take_ctx(0)
                    for c in range(TT):
                        if c + 1 < TT:
                            take_ctx(c + 1)
                        take_k(c)

            def take_max(u, g):
                act.wait_ge(mxT_ps, u + 1)
                act.activation(q2_op[0:PARTS, g, :], bank(6 + g % 2)[:, :].bitcast(bf16)[0:PARTS, :], ACT.Copy).then_inc(mxT_sb, 1)

            def unit(i, g, last):
                for t in range(KT):
                    step = KT * (G * i + g) + t
                    r = key_rows(t)
                    slot = (KT * g + t) % 4
                    for h in range(2):
                        if h == 0:
                            act.wait_ge(pv_done, step + 1)
                        act.wait_ge(s2_ready, 2 * step + h + 1)
                        act.activation(pt[0:r, slot, h * BANK:(h + 1) * BANK], bank(4 + h)[0:r, :], ACT.Exp).then_inc(exp_done, 1)
                    if t == MX_STEP + 1 and not (last and g == G - 1):
                        take_max(G * i + g + 1, (g + 1) % G)

            take_max(0, 0)
            with act.Fori(0, B - 1) as i:
                for g in range(G):
                    unit(i, g, False)
            for g in range(G):
                unit(B - 1, g, True)

            act.wait_ge(o_done, B * G + 4)
            with act.Fori(0, B // 2) as i:
                for p in range(2):
                    b = 2 * i + p
                    act.wait_ge(xT2_ps, b + 1)
                    act.activation(x_nT[:, p, :], bank(3)[:, 0:S], ACT.Copy).then_inc(xT2_sb, 1)
                    for c in range(FC):
                        if c % 2 == 0:
                            act.wait_ge(h_ps, FC // 2 * b + c // 2 + 1)
                        act.activation(hT[:, p, c, :], bank(4 + c // 2)[:, (c % 2) * S:(c % 2 + 1) * S], ACT.Gelu,
                                       bias=b_fc[:, c:c + 1]).then_inc(h_sb, 1)

        @block.vector
        def _(dve):
            n = [0]

            def link(ins):
                n[0] += 1
                ins.then_inc(dve_chain, 1)
                dve.wait_ge(dve_chain, n[0])

            nc.vector.memset(w_o[:, :, :], 0.0).then_inc(wq_ready, 1)
            for s_, d_ in ((ctxT_sb, 2), (k_ev, 2), (v_ps, 8), (v_ev, 2), (k_split, 2), (pv_done, 4), (o_done, 4),
                           (kv_stored[0], 80), (kv_stored[1], 80), (out_stored[0], 16), (out_stored[1], 16), (otn_sb, 1)):
                dve.sem_inc(s_, d_)
            def bc(ap):
                return ap.unsqueeze(2).to_broadcast([P, B * QT, D])
            dve.wait_ge(x_loaded, 16)
            link(nc.vector.reduce_sum(ln_sum[:, :], x_sb[:, :, :], AX.X))
            link(nc.vector.tensor_scalar(ln_mean[:, :], ln_sum[:, :], 1.0 / D, None, ALU.mult))
            link(nc.vector.tensor_tensor(qc[:, :, :], x_sb[:, :, :], bc(ln_mean[:, :]), ALU.subtract))
            link(nc.vector.tensor_tensor(qsq[:, :, :], qc[:, :, :], qc[:, :, :], ALU.mult))
            nc.vector.reduce_sum(ln_var[:, :], qsq[:, :, :], AX.X).then_inc(ln_ready, 1)
            dve.wait_ge(mask_loaded, 32)
            link(nc.vector.tensor_scalar(mask0[:, :], mask0[:, :], -BIG, BIG, ALU.max, ALU.min))
            nc.vector.tensor_scalar(mask_q[:, :, :], mask_q[:, :, :], -BIG, BIG, ALU.max, ALU.min).then_inc(clamp, 1)
            dve.wait_ge(rstd_ready, 1)
            nc.vector.tensor_tensor(qn[:, :, :], qc[:, :, :], bc(ln_rstd[:, :]), ALU.mult).then_inc(xn_ready, 1)
            link(nc.vector.tensor_copy(m0_hi[0:1, 0:KEYS], mask0[0:1, :]))
            link(nc.vector.tensor_tensor(m0_res[0:1, :], mask0[0:1, :], m0_hi[0:1, 0:KEYS], ALU.subtract))
            link(nc.vector.tensor_copy(m0_hi[0:1, KEYS:2 * KEYS], m0_res[0:1, :]))
            nc.vector.tensor_tensor(m0_hi[0:1, 2 * KEYS:3 * KEYS], m0_res[0:1, :], m0_hi[0:1, KEYS:2 * KEYS], ALU.subtract).then_inc(m0_split, 1)
            dve.wait_ge(clamp, 1)
            flat = qsq[:, :, :].rearrange("p t d -> p (t d)")
            for t in range(QT):
                link(nc.vector.tensor_tensor(flat[:, 0:KEYS], mask_q[:, t, :], mask0[:, :], ALU.not_equal))
                link(nc.vector.tensor_reduce(rng[:, t:t + 1], flat[:, 0:KEYS], AX.X, ALU.max))
            link(nc.vector.reduce_max(rng[:, 2:3], mask0[:, :], AX.X))
            link(nc.vector.tensor_scalar(rng[:, 3:4], rng[:, 2:3], PLAIN_TOP, None, ALU.is_gt))
            link(nc.vector.tensor_scalar(rng[:, 2:3], rng[:, 2:3], -PLAIN_TOP, None, ALU.is_lt))
            link(nc.vector.tensor_reduce(stat[:, 2:3], rng[:, :], AX.X, ALU.max))
            dve.wait_ge(ffn_loaded, 160)
            link(nc.vector.tensor_reduce(stat[:, 0:1], wf_in, AX.X, ALU.max, apply_absolute_value=True))
            nc.vector.tensor_reduce(stat[:, 1:2], wp_in, AX.X, ALU.max, apply_absolute_value=True).then_inc(stat_ready, 1)
            dve.wait_ge(stat_ps, 1)
            link(nc.vector.reduce_max(stat_t[:, :], bank(5)[0:PARTS, 0:P], AX.X))
            nc.vector.tensor_scalar(stat_d[:, :], ident[0:PARTS, 0:PARTS], stat_t[:, 0:1], None, ALU.mult).then_inc(stat_diag, 1)
            dve.wait_ge(stat_ps, 2)
            link(nc.vector.tensor_copy(allstat[:, :], bank(5)[:, 0:PARTS]))
            link(nc.vector.tensor_scalar(plain[:, :], allstat[:, 2:3], -1.0, 1.0, ALU.mult, ALU.add))
            nc.vector.tensor_copy(general_i[:, :], allstat[0:1, 2:3]).then_inc(flag_ready, 1)
            link(nc.vector.tensor_scalar(inv_s[:, 0:2], allstat[:, 0:2], 1.0 / QMAX, None, ALU.mult))
            link(nc.vector.reciprocal(inv_s[:, 2:4], inv_s[:, 0:2]))
            for k, (w, r_) in enumerate(((wf_in, wf_r), (wp_in, wp_r))):
                link(nc.vector.tensor_scalar(wf_a, w, inv_s[:, 2 + k:3 + k], MAGIC, ALU.mult, ALU.add))
                link(nc.vector.tensor_scalar(wf_b, wf_a, -MAGIC, -QMAX - 1.0, ALU.add, ALU.max))
                link(nc.vector.tensor_scalar(wf_a, wf_b, QMAX, inv_s[:, k:k + 1], ALU.min, ALU.mult))
                link(nc.vector.tensor_tensor(wf_b, wf_a, w, ALU.subtract))
                nc.vector.tensor_tensor(r_, wf_b, w, ALU.add).then_inc(wq_ready, 1)
                dve.wait_ge(wq_ready, 2 + k)
            dve.wait_ge(q_ev, 4)
            nc.vector.tensor_tensor(q_res[:, :], q_full[:, :], q_bf[:, 0, :], ALU.subtract).then_inc(q_split, 1)
            dve.wait_ge(q_split, 1)
            nc.vector.tensor_copy(q_bf[:, 1, :], q_res[:, :]).then_inc(q_split, 1)
            dve.wait_ge(q_split, 2)
            nc.vector.tensor_tensor(q_bf[:, 2, :], q_res[:, :], q_bf[:, 1, :], ALU.subtract).then_inc(q_split, 1)
            dve.wait_ge(ext_in, 48)
            dve.wait_ge(consts, 7)
            nc.vector.tensor_scalar(extf[:, :], ext[:, :], plain[0:XR, 0:1], None, ALU.mult).then_inc(ext_flag, 1)

            dve.wait_ge(q_stored, 16 * TERMS)
            dve.wait_ge(mT_split, 4)
            dve.wait_ge(q_ps, 4)
            ksub = sem("ksub")
            with dve.Fori(0, B // 2) as i:
                for p in range(2):
                    b = 2 * i + p
                    dve.wait_ge(kv_stored[p], 80 * (i + 1))
                    for c in range(TT):
                        dve.wait_ge(v_ps, TT * b + c + 1 + 8)
                        tiles = min(4, KT - 4 * c)
                        rows = P if tiles == 4 else TAIL
                        nc.vector.tensor_tensor(v_out[0:rows, p, 4 * c:4 * c + tiles, :],
                                                bank(4 + c % 2)[0:rows, 0:tiles * D].rearrange("p (t d) -> p t d", d=D),
                                                bv_all[0:rows, :].unsqueeze(1).to_broadcast([rows, tiles, D]),
                                                ALU.add).then_inc(v_ev, 1)
                    dve.wait_ge(k_ev, TT * (b + 1) + 2)
                    nc.vector.tensor_tensor(k_res[:, :], k_full[:, p, :], k_pool[:, p, 0, :], ALU.subtract).then_inc(ksub, 1)
                    dve.wait_ge(ksub, 2 * b + 1)
                    nc.vector.tensor_copy(k_pool[:, p, 1, :], k_res[:, :]).then_inc(ksub, 1)
                    dve.wait_ge(ksub, 2 * b + 2)
                    nc.vector.tensor_tensor(k_pool[:, p, 2, :], k_res[:, :], k_pool[:, p, 1, :], ALU.subtract).then_inc(k_split, 1)

            def chunk(i, g, c):
                u = G * i + g
                qh, half = c // 2, c % 2
                lo = half * HALF
                width = min(HALF, KEYS - lo)
                pos = CHUNKS * u + c
                two = ps[:, 2 * half:2 * half + 2, :].rearrange("p a n -> p (a n)")
                settled(dve, s1_ready, pos + 1)
                nc.vector.tensor_tensor_reduce(out=two[:, 0:width], in0=two[:, 0:width],
                                               in1=mask_q[:, qh % QT, lo:lo + width], scale=1.0, scalar=-3.4e38,
                                               op0=ALU.add, op1=ALU.max,
                                               accum_out=mx_part[:, g % 2, qh, half:half + 1]).then_inc(s1_done, 1)
                if c == CHUNKS - 1:
                    dve.wait_ge(s1_done, pos + 1)
                    nc.vector.tensor_reduce(mx_neg[:, g % 2, :], mx_part[:, g % 2, :, :], AX.X, ALU.max,
                                            negate=True).then_inc(mx_ready, 1)

            def unit(i, g, last):
                for t in range(KT):
                    for c in range(chunk_pos(t + LEAD), chunk_pos(t + 1 + LEAD)):
                        ahead = g + 1 + c // CHUNKS
                        if not (last and ahead >= G):
                            chunk(i, ahead, c % CHUNKS)
                u = G * i + g
                dve.wait_ge(pv_done, KT * (u + 1) + 4)
                nc.vector.tensor_copy(ot[:, bass.ds(u, 1), :] if not last else ot[:, u:u + 1, :],
                                      bank(6 + g % 2)[:, 0:S].unsqueeze(1)).then_inc(o_done, 1)

            for c in range(CHUNKS):
                chunk(0, 0, c)
            for c in range(chunk_pos(LEAD)):
                chunk(0, 1, c)
            with dve.Fori(0, B - 1) as i:
                for g in range(G):
                    unit(i, g, False)
            for g in range(G):
                unit(B - 1, g, True)

            e1 = sem("e1")
            e2 = sem("e2")
            dve.wait_ge(o_done, B * G + 4)

            def attend(b, p):
                for k in range(2):
                    dve.wait_ge(r_ps, 2 * b + k + 1)
                    inv = junk[:, 0:BANK]
                    dve.wait_ge(otn_sb, 2 * b + k + 1)
                    nc.vector.reciprocal(inv, bank(k)).then_inc(r_inv, 1)
                    dve.wait_ge(r_inv, 2 * b + k + 1)
                    nc.vector.tensor_tensor(otn[:, p, 2 * k:2 * k + 2, :],
                                            ot[:, bass.ds(G * b + 2 * k, 2), :],
                                            inv.rearrange("p (g s) -> p g s", g=2), ALU.mult).then_inc(otn_sb, 1)
                dve.wait_ge(y_ps, b + 1)
                nc.vector.scalar_tensor_tensor(out=x_mid[:, p, :, :], in0=bank(2)[:, 0:QT * D].rearrange("p (t d) -> p t d", t=QT),
                                               scalar=tgates[:, 0:1], in1=x_sb[:, bass.ds(QT * b, QT), :],
                                               op0=ALU.mult, op1=ALU.add).then_inc(mid_ready, 1)
                dve.wait_ge(mid_ready, b + 1)
                nc.vector.reduce_sum(l_sum[:, p, :], x_mid[:, p, :, :], AX.X).then_inc(e1, 1)
                dve.wait_ge(e1, 4 * b + 1)
                nc.vector.tensor_scalar(l_sum[:, p, :], l_sum[:, p, :], 1.0 / D, None, ALU.mult).then_inc(e1, 1)
                dve.wait_ge(e1, 4 * b + 2)
                nc.vector.tensor_tensor(x_c[:, p, :, :], x_mid[:, p, :, :],
                                        l_sum[:, p, :].unsqueeze(2).to_broadcast([P, QT, D]), ALU.subtract).then_inc(e1, 1)
                dve.wait_ge(e1, 4 * b + 3)
                nc.vector.tensor_tensor(x_n[:, p, :, :], x_c[:, p, :, :], x_c[:, p, :, :], ALU.mult).then_inc(e1, 1)
                dve.wait_ge(e1, 4 * b + 4)
                nc.vector.reduce_sum(l_sum[:, p, :], x_n[:, p, :, :], AX.X).then_inc(mid_sum, 1)
                nc.vector.scalar_tensor_tensor(out=x_res[:, p, :, :],
                                               in0=b_pj[:, :].unsqueeze(1).to_broadcast([P, QT, D]),
                                               scalar=tgates[:, 1:2], in1=x_mid[:, p, :, :],
                                               op0=ALU.mult, op1=ALU.add).then_inc(e2, 1)
                dve.wait_ge(mid_rstd, 2 * b + 2)
                nc.vector.tensor_tensor(x_n[:, p, :, :], x_c[:, p, :, :],
                                        l_rstd[:, p, :].unsqueeze(2).to_broadcast([P, QT, D]), ALU.mult).then_inc(xn2_ready, 1)

            def finish(b, p, i):
                dve.wait_ge(e2, b + 1)
                dve.wait_ge(out_stored[p], 16 * (i + 1))
                for t in range(QT):
                    dve.wait_ge(out_ps, QT * b + t + 1)
                    nc.vector.scalar_tensor_tensor(out=out_sb[:, p, t, :], in0=bank(6 + t)[:, 0:D],
                                                   scalar=tgates[:, 1:2], in1=x_res[:, p, t, :],
                                                   op0=ALU.mult, op1=ALU.add).then_inc(out_ready, 1)

            with dve.Fori(0, B // 2) as i:
                for p in range(2):
                    attend(2 * i + p, p)
                    finish(2 * i + p, p, i)

        @block.tensor
        def _(pe):
            pe.wait_ge(consts, 7)
            pe.wait_ge(ffn_loaded, 160)
            for c in range(FC):
                m = nc.tensor.transpose(bank(7)[0:RANK, c * P:(c + 1) * P], bl_fc[:, c, :], ident[:, :])
            m.then_inc(lora_ps, 1)
            nc.tensor.transpose(bank(6)[0:RANK, 0:P], bl_pj[:, :], ident[:, :]).then_inc(lora_ps, 1)
            pe.wait_ge(xn_ready, 1)
            for c in range(4):
                for k in range(4):
                    m = nc.tensor.transpose(bank(c)[:, k * P:(k + 1) * P], qn[:, 4 * c + k, :], ident[:, :])
                m.then_inc(xnT_ps, 1)
            pe.wait_ge(proj_loaded, 96)
            for c in range(4):
                pe.wait_ge(xnT_sb, c + 1)
                nc.tensor.matmul(bank(c), w_qkv[:, 0, :], xnT[:, c * BANK:(c + 1) * BANK], start=True, stop=True).then_inc(q_ps, 1)
            pe.wait_ge(clamp, 1)
            for t in range(KT):
                r = key_rows(t)
                if t >= 2:
                    pe.wait_ge(mT_sb, t - 1)
                for k in range(QT):
                    m = nc.tensor.transpose(bank(4 + t % 2)[0:r, k * P:(k + 1) * P], mask_q[:, k, t * P:t * P + r], ident[:, :])
                m.then_inc(mT_ps, 1)
            pe.wait_ge(stat_ready, 1)
            pe.wait_ge(mT_sb, KT)
            nc.tensor.transpose(bank(5)[0:PARTS, 0:P], stat[:, :], ident[:, :]).then_inc(stat_ps, 1)
            pe.wait_ge(stat_diag, 1)
            nc.tensor.matmul(bank(5)[:, 0:PARTS], ones_f[:, :], stat_d[:, :], start=True, stop=True).then_inc(stat_ps, 1)
            pe.wait_ge(lora_sb, 2)
            pe.wait_ge(wq_ready, 2)
            for c in range(FC):
                cs = slice(c * P, (c + 1) * P)
                nc.tensor.matmul(bank(6)[:, cs], wf_r[:, cs], ident[:, :], start=True, stop=False)
                m = nc.tensor.matmul(bank(6)[:, cs], a_fc[:, :], blT_fc[:, cs], start=False, stop=True)
            m.then_inc(weff_ps, 1)
            pe.wait_ge(wq_ready, 3)
            for c in range(FC):
                cs = slice(c * P, (c + 1) * P)
                nc.tensor.matmul(bank(7)[:, cs], wp_r[:, cs], ident[:, :], start=True, stop=False)
                m = nc.tensor.matmul(bank(7)[:, cs], a_pj[:, cs], blT_pj[:, :], start=False, stop=True)
            m.then_inc(weff_ps, 1)

            pe.wait_ge(q_ev, 4)
            pe.wait_ge(stat_ps, 2)
            pe.wait_ge(flag_ready, 1)
            with pe.Fori(0, B // 2) as i:
                for p in range(2):
                    b = 2 * i + p

                    def turn(c):
                        pe.wait_ge(ctxT_sb, TT * b + c + 1)
                        for t in range(4 * c, min(4 * c + 4, KT)):
                            r = key_rows(t)
                            m = nc.tensor.transpose(bank(c % 2)[:, (t % 4) * P:(t % 4) * P + r], ctx_in[0:r, p, t, :], ident[0:r, 0:r])
                        m.then_inc(ctxT_ps, 1)

                    def project(c):
                        n_ = TT * b + c
                        lo, hi = CH[c]
                        pe.wait_ge(ctxT_sb, n_ + 1 + 2)
                        pe.wait_ge(k_ev, n_ + 1)
                        nc.tensor.matmul(bank(2 + c % 2)[:, 0:hi - lo], w_qkv[:, 1, :], ctxT[:, p, lo:hi],
                                         start=True, stop=True).then_inc(k_ps, 1)
                        pe.wait_ge(v_ev, n_ + 1)
                        for t in range(4 * c, min(4 * c + 4, KT)):
                            r = key_rows(t)
                            m = nc.tensor.matmul(bank(4 + c % 2)[0:r, (t % 4) * D:(t % 4 + 1) * D],
                                                 ctxT[:, p, t * P:t * P + r], w_qkv[:, 2, :], start=True, stop=True)
                        m.then_inc(v_ps, 1)

                    pe.wait_ge(ctx_loaded[p], 32 * (i + 1))
                    turn(0)
                    for c in range(TT):
                        if c + 1 < TT:
                            turn(c + 1)
                        project(c)

            general = pe.value_load(general_i[0:1, 0:1], min_val=0, max_val=1)

            def chunk(i, g, c):
                u = G * i + g
                slot = g % G
                qh, half = c // 2, c % 2
                h, qt = qh // QT, qh % QT
                lo = half * HALF
                width = min(HALF, KEYS - lo)
                pos = CHUNKS * u + c
                if c == 0:
                    pe.wait_ge(kq_loaded[slot], 80 * (i + g // G + 1))
                if not (isinstance(i, int) and pos < 2):
                    pe.wait_ge(s1_done, pos - 1)
                for k, (a, z) in enumerate(cuts(width)):
                    m = nc.tensor.matmul(ps[:, 2 * half + k, 0:z - a], q1_op[:, slot, h, qt * P:(qt + 1) * P],
                                         kv_k[0:KR, slot, h, lo + a:lo + z], start=True, stop=True)
                m.then_inc(s1_ready, 1)

            def turn_max(u, slot):
                pe.wait_ge(mx_split, 4 * (u + 1))
                pe.wait_ge(o_done, u + 3)
                rows = bank(6 + slot % 2)[:, :].bitcast(bf16)
                for j in range(HG * QT):
                    m = nc.tensor.transpose(rows[0:PARTS, j * P:(j + 1) * P], mx_bf[:, slot % 2, j, :], identb[:, :])
                m.then_inc(mxT_ps, 1)

            def sweep2(i, g, t, arm):
                slot = g % G
                step = KT * (G * i + g) + t
                r = key_rows(t)
                if t == 0:
                    pe.wait_ge(mxT_sb, G * i + g + 1)
                for k in range(2):
                    if not (isinstance(i, int) and step == 0):
                        pe.wait_ge(exp_done, 2 * step + k - 1)
                    out = bank(4 + k)[0:r, :]
                    if arm == "general":
                        for a in range(PARTS):
                            nc.tensor.matmul(out.rearrange("p (h s) -> p h s", h=2), identb[0:r, 0:r],
                                             maskT[0:r, t, a, :].unsqueeze(1).to_broadcast([r, 2, S]),
                                             start=(a == 0), stop=False)
                    for h in range(2 * k, 2 * k + 2):
                        m = nc.tensor.matmul(out[:, (h % 2) * S:(h % 2 + 1) * S], kv_k[0:KR, slot, h, t * P:t * P + r],
                                             q2_op[:, slot, h * S:(h + 1) * S],
                                             start=(arm != "general"), stop=(arm != "general"))
                    if arm == "general":
                        m = nc.tensor.matmul(out, ones_m[:, 0:r], q2_op[:, slot, 2 * k * S:(2 * k + 2) * S],
                                             start=False, stop=True)
                    m.then_inc(s2_ready, 1)

            def multiply_v(i, g, t):
                step = KT * (G * i + g) + t
                r = key_rows(t)
                if t == 0:
                    pe.wait_ge(v_op_ready, G * i + g + 1)
                pe.wait_ge(exp_done, 2 * step + 2)
                for h in range(HG):
                    m = nc.tensor.matmul(bank(6 + g % 2)[32 * h:32 * h + 32, 0:S], v_op[0:r, g, t, h, :],
                                         pt[0:r, (KT * g + t) % 4, h * S:(h + 1) * S],
                                         start=(t == 0), stop=(t == KT - 1))
                m.then_inc(pv_done, 1)

            def unit(i, g, last, arm):
                for t in range(KT):
                    final = last and g == G - 1
                    if t + 1 < KT:
                        sweep2(i, g, t + 1, arm)
                    elif not final:
                        sweep2(i, g + 1, 0, arm)
                    if t == MX_STEP and not final:
                        turn_max(G * i + g + 1, (g + 1) % G)
                    for c in range(chunk_pos(t + LEAD), chunk_pos(t + 1 + LEAD)):
                        ahead = g + 1 + c // CHUNKS
                        if not (last and ahead >= G):
                            chunk(i, ahead, c % CHUNKS)
                    multiply_v(i, g, t)

            def either(body):
                with pe.If(general != 0):
                    body("general")
                with pe.Else():
                    body("plain")

            pe.wait_ge(ext_out, 64)
            for c in range(CHUNKS):
                chunk(0, 0, c)
            for c in range(chunk_pos(LEAD)):
                chunk(0, 1, c)
            turn_max(0, 0)
            either(lambda arm: sweep2(0, 0, 0, arm))
            with pe.Fori(0, B - 1) as i:
                either(lambda arm: [unit(i, g, False, arm) for g in range(G)])
            either(lambda arm: [unit(B - 1, g, True, arm) for g in range(G)])

            pe.wait_ge(o_done, B * G + 4)
            pe.wait_ge(wo_loaded, 80)

            def attend(b, p):
                for k in range(2):
                    nc.tensor.matmul(bank(k).rearrange("p (g s) -> p g s", g=2), sel[:, :], ot[:, bass.ds(G * b + 2 * k, 2), :],
                                     start=True, stop=True).then_inc(r_ps, 1)
                pe.wait_ge(otn_sb, 2 * b + 2 + 1)
                for t in range(QT):
                    for g in range(G):
                        m = nc.tensor.matmul(bank(2)[:, t * D:(t + 1) * D], otn[:, p, g, t * P:(t + 1) * P], w_o[:, g, :],
                                             start=(g == 0), stop=(g == G - 1))
                m.then_inc(y_ps, 1)

            def ffn(b, p):
                pe.wait_ge(xn2_ready, b + 1)
                for t in range(QT):
                    m = nc.tensor.transpose(bank(3)[:, t * P:(t + 1) * P], x_n[:, p, t, :], ident[:, :])
                m.then_inc(xT2_ps, 1)
                pe.wait_ge(xT2_sb, b + 1)
                for c in range(FC):
                    m = nc.tensor.matmul(bank(4 + c // 2)[:, (c % 2) * S:(c % 2 + 1) * S], w_fcT[:, c * P:(c + 1) * P],
                                         x_nT[:, p, :], start=True, stop=True)
                    if c % 2:
                        m.then_inc(h_ps, 1)
                for t in range(QT):
                    for c in range(FC):
                        pe.wait_ge(h_sb, FC * b + c + 1)
                        m = nc.tensor.matmul(bank(6 + t)[:, 0:D], hT[:, p, c, t * P:(t + 1) * P], w_pjT[:, c, :],
                                             start=(c == 0), stop=(c == FC - 1))
                    m.then_inc(out_ps, 1)

            with pe.Fori(0, B // 2) as i:
                for p in range(2):
                    attend(2 * i + p, p)
                    ffn(2 * i + p, p)


_INS = ['x', 'ctx_1024', 'mask_SxS2_fk0', 'g_xattn', 'g_ffn', 'L0_xattn_Wq', 'L0_xattn_bq', 'L0_xattn_Wk', 'L0_xattn_bk',
        'L0_xattn_Wv', 'L0_xattn_bv', 'L0_xattn_Wo', 'L0_xattn_bo', 'L0_ffn_W_fc', 'L0_ffn_b_fc', 'L0_ffn_A_fc',
        'L0_ffn_B_fc', 'L0_ffn_W_proj', 'L0_ffn_b_proj', 'L0_ffn_A_proj', 'L0_ffn_B_proj']


def kernel(**inputs):
    import numpy as _np
    import concourse.bacc as _bacc
    from concourse import mybir as _mybir
    from concourse.bass_utils import run_bass_kernel_spmd as _run

    nc = _bacc.Bacc("TRN2", target_bir_lowering=False, num_devices=1)
    arrays, io = {}, {}
    for name in _INS:
        a = _np.ascontiguousarray(inputs[name])
        arrays[f"in_{name}"] = a
        io[name] = nc.dram_tensor(f"in_{name}", a.shape, _mybir.dt.from_np(a.dtype), kind="ExternalInput").ap()
    shape = arrays["in_x"].shape
    io["out"] = nc.dram_tensor("out_0", shape, _mybir.dt.float32, kind="ExternalOutput").ap()
    flamingo_block(nc, io)
    r = _run(nc, [arrays], core_ids=[0])
    return r.results[0]["out_0"]
```

```python
import concourse.bass as bass
from concourse import mybir
from contextlib import ExitStack


def flamingo_block(nc, io):
    fp32, bf16, i32 = mybir.dt.float32, mybir.dt.bfloat16, mybir.dt.int32
    ALU = mybir.AluOpType
    ACT = mybir.ActivationFunctionType
    AX = mybir.AxisListType

    B, S, D = io["x"].shape
    KEYS = io["ctx_1024"].shape[1]
    F = io["L0_ffn_W_fc"].shape[0]
    RANK = io["L0_ffn_A_fc"].shape[0]
    P = 128
    NH, HD = 16, D // 16
    HG = 4
    G = NH // HG
    QT = S // P
    KT = -(-KEYS // P)
    TAIL = KEYS - (KT - 1) * P
    BANK = 512
    HALF = (KEYS + 1) // 2
    PARTS = 3
    K_PART = [0, 1, 2, 0, 1, 0]
    Q_PART = [0, 0, 0, 1, 1, 2]
    TERMS = len(K_PART)
    TR = TERMS * HD
    XR = 2 * PARTS
    KR = XR + TR
    FC = F // P
    TOK = B * S
    QSCALE = float(HD) ** -0.5
    BIG = 3.0e38
    PLAIN_TOP = 1024.0
    EPS = 1e-5
    QMAX = 127.0
    MAGIC = 1.5 * 2.0 ** 23
    CHUNKS = 2 * QT * HG
    LEAD = 5
    O_STEP, OT_STEP, Y_STEP = 2, 5, 7
    LN_STEPS = (0, 2, 4, 6, 8, 12)
    MX_STEP = 10

    def key_rows(t):
        return P if t < KT - 1 else TAIL

    def settled(eng, sem_, value):
        eng.wait_ge(sem_, value)
        eng.sem_inc(passed, 1)

    def cuts(width):
        return [(a, min(a + BANK, width)) for a in range(0, width, BANK)]

    with ExitStack() as ctx:
        def sb(name, shape, dt):
            return ctx.enter_context(nc.sbuf_tensor(name, shape, dt))

        def sem(name):
            return ctx.enter_context(nc.semaphore(name))

        ps = ctx.enter_context(nc.psum_tensor("ps", [P, 8, BANK], fp32))

        def bank(n):
            return ps[:, n, :]

        k_op = sb("k_op", [P, G * HG * KEYS], bf16)
        q1_op = sb("q1_op", [P, G, HG, S], bf16)
        q2_op = sb("q2_op", [P, G, HG * S], bf16)
        v_in = sb("v_in", [P, KT, D], fp32)
        v_op = sb("v_op", [P, G, KT, HG, 32], fp32)
        mask_q = sb("mask_q", [P, QT, KEYS], fp32)
        maskT = sb("maskT", [P, KT, PARTS, S], bf16)
        x_all = sb("x_all", [P, QT + B * QT, D], fp32)
        x_sb = x_all[:, QT:, :]
        work = sb("work", [P, B * G * S], fp32)
        pt = sb("pt", [P, 4, HG * S], fp32)
        junk = sb("junk", [P, HALF], fp32)
        w_qkv = sb("w_qkv", [P, 3, D], fp32)
        b_qk = sb("b_qk", [P, 3], fp32)
        bv_all = sb("bv_all", [P, D], fp32)
        w_o = sb("w_o", [P, D], fp32)
        bo_all = sb("bo_all", [P, D], fp32)
        ident = sb("ident", [P, P], fp32)
        identb = sb("identb", [P, P], bf16)
        ones_m = sb("ones_m", [P, P], bf16)
        ones_f = sb("ones_f", [PARTS, P], fp32)
        gates = sb("gates", [P, 2], fp32)
        tgates = sb("tgates", [P, 2], fp32)
        stat = sb("stat", [P, PARTS], fp32)
        rng = sb("rng", [P, 4], fp32)
        stat_t = sb("stat_t", [PARTS, 1], fp32)
        stat_d = sb("stat_d", [PARTS, PARTS], fp32)
        allstat = sb("allstat", [P, PARTS], fp32)
        plain = sb("plain", [P, 1], fp32)
        general_i = sb("general_i", [1, 1], i32)
        half_neg = sb("half_neg", [P, B * QT], fp32)
        ln_sum = sb("ln_sum", [P, B * QT], fp32)
        ln_mean = sb("ln_mean", [P, B * QT], fp32)
        ln_var = sb("ln_var", [P, B * QT], fp32)
        ln_rstd = sb("ln_rstd", [P, B * QT], fp32)
        mx_part = sb("mx_part", [P, 2, HG * QT, 2], fp32)
        mx_neg = sb("mx_neg", [P, 2, HG * QT], fp32)
        mx_res = sb("mx_res", [P, 2, HG * QT], fp32)
        mx_bf = sb("mx_bf", [P, 2, HG * QT, PARTS], bf16)
        w_fcT = sb("w_fcT", [P, F], fp32)
        w_pjT = sb("w_pjT", [P, FC, D], fp32)
        b_fc = sb("b_fc", [P, FC], fp32)
        b_pj = sb("b_pj", [P, D], fp32)
        l_sum = sb("l_sum", [P, QT], fp32)
        l_mean = sb("l_mean", [P, QT], fp32)
        l_var = sb("l_var", [P, QT], fp32)
        l_rstd = sb("l_rstd", [P, QT], fp32)

        kv_k = k_op[:, :].rearrange("p (g h k) -> p g h k", g=G, h=HG)
        off = 2 * HG * KEYS
        k_pool = k_op[:, off:off + 2 * PARTS * KEYS].rearrange("p (b a k) -> p b a k", b=2, a=PARTS)
        v_flat = v_op[:, :, :, :, :].rearrange("p g t h c -> p (g t h c)")
        v_out = v_flat[:, 0:2 * KT * D].rearrange("p (b t d) -> p b t d", b=2, t=KT)
        k_res = v_flat[:, 2 * KT * D:2 * KT * D + KEYS]
        ot_flat = work[:, :]
        ctx_in = ot_flat[:, 0:2 * KT * D].rearrange("p (b t d) -> p b t d", b=2, t=KT)
        ctxT = ot_flat[:, 2 * KT * D:2 * KT * D + 2 * KEYS].rearrange("p (b k) -> p b k", b=2)
        pt_flat = pt[:, :, :].rearrange("p n s -> p (n s)")
        k_full = pt_flat[:, 0:2 * KEYS].rearrange("p (b k) -> p b k", b=2)
        qn = ot_flat[:, 0:TOK].rearrange("p (t d) -> p t d", d=D)
        qc = ot_flat[:, TOK:2 * TOK].rearrange("p (t d) -> p t d", d=D)
        qsq = ot_flat[:, 2 * TOK:3 * TOK].rearrange("p (t d) -> p t d", d=D)
        xnT = ot_flat[:, 3 * TOK:4 * TOK]
        q_full = pt_flat[:, 0:TOK]
        q_res = pt_flat[:, TOK:2 * TOK]
        q_bf = k_op[:, 0:PARTS * TOK].rearrange("p (a s) -> p a s", a=PARTS)
        m_off = PARTS * TOK
        mT_full = k_op[:, m_off:m_off + 2 * KT * S].bitcast(fp32)
        mT_res = k_op[:, m_off + 2 * KT * S:m_off + 4 * KT * S].bitcast(fp32)
        mask0 = v_in[:, :, :].rearrange("p t d -> p (t d)")[:, 0:KEYS]
        m0_off = m_off + 4 * KT * S
        m0_hi = k_op[:, m0_off:m0_off + PARTS * KEYS]
        m0_res = q_res[:, 0:KEYS]
        extf = junk[:, :].bitcast(bf16)[0:XR, 0:KEYS]
        ext = v_op[0:XR, 2, 4:KT, :, :].rearrange("p t h c -> p (t h c)").bitcast(bf16)[:, 0:KEYS]
        wf_in = v_op[:, 0, 0:4, :, :].rearrange("p t h c -> p (t h c)")
        wp_in = v_op[:, 1, 0:4, :, :].rearrange("p t h c -> p (t h c)")
        wf_a = v_op[:, 2, 0:4, :, :].rearrange("p t h c -> p (t h c)")
        wf_b = v_op[:, 3, 0:4, :, :].rearrange("p t h c -> p (t h c)")
        wf_r = v_in[:, 0:4, :].rearrange("p t d -> p (t d)")
        wp_r = v_in[:, 4:8, :].rearrange("p t d -> p (t d)")
        o_inv = sb("o_inv", [P, QT, HG], fp32)
        inv_s = sb("inv_s", [P, 4], fp32)
        a_fc = sb("a_fc", [RANK, D], fp32)
        bl_fc = sb("bl_fc", [P, FC, RANK], fp32)
        a_pj = v_op[0:RANK, 0, 4:8, :, :].rearrange("p t h c -> p (t h c)")
        bl_pj = sb("bl_pj", [P, RANK], fp32)
        blT_fc = v_op[0:RANK, 1, 4:8, :, :].rearrange("p t h c -> p (t h c)")
        blT_pj = sb("blT_pj", [RANK, D], fp32)
        out_sb = v_flat[:, 0:2 * QT * D].rearrange("p (b t d) -> p b t d", b=2, t=QT)
        x_nT = v_flat[:, 2 * QT * D:4 * QT * D].rearrange("p (b s) -> p b s", b=2)
        x_nS = v_flat[:, 4 * QT * D:6 * QT * D].rearrange("p (b t d) -> p b t d", b=2, t=QT)
        x_res = v_flat[:, 6 * QT * D:8 * QT * D].rearrange("p (b t d) -> p b t d", b=2, t=QT)
        hT = pt_flat[:, 0:2 * FC * S].rearrange("p (b c s) -> p b c s", b=2, c=FC)
        o_raw = work[:, 0:2 * S].rearrange("p (b s) -> p b s", b=2)
        o_q = work[:, 2 * S:2 * S + QT * D].rearrange("p (t d) -> p t d", t=QT)
        w0 = 2 * S + QT * D
        oT = work[:, w0:w0 + S]
        w0 = w0 + S
        x_c = work[:, w0:w0 + QT * D].rearrange("p (t d) -> p t d", t=QT)
        x_q = work[:, w0 + QT * D:w0 + 2 * QT * D].rearrange("p (t d) -> p t d", t=QT)
        w1 = w0 + 2 * QT * D
        x_n = work[:, w1:w1 + (1 + B) * QT * D].rearrange("p (t d) -> p t d", d=D)

        k_scr = nc.dram_tensor("k_scr", [B, NH, PARTS, HD, KEYS], bf16, kind="Internal").ap()
        q_scr = nc.dram_tensor("q_scr", [NH, TERMS, HD, B * S], bf16, kind="Internal").ap()
        v_scr = nc.dram_tensor("v_scr", [B, KT, P, D], fp32, kind="Internal").ap()

        passed = sem("passed")
        x_loaded = sem("x_loaded")
        proj_loaded = sem("proj_loaded")
        mask_loaded = sem("mask_loaded")
        ffn_loaded = sem("ffn_loaded")
        wo_loaded = sem("wo_loaded")
        consts = sem("consts")
        pool_chain = sem("pool_chain")
        dve_chain = sem("dve_chain")
        act_chain = sem("act_chain")
        tanh_ready = sem("tanh_ready")
        ln_ready = sem("ln_ready")
        rstd_ready = sem("rstd_ready")
        xn_ready = sem("xn_ready")
        xnT_ps = sem("xnT_ps")
        xnT_sb = sem("xnT_sb")
        q_ps = sem("q_ps")
        q_ev = sem("q_ev")
        q_split = sem("q_split")
        q_stored = sem("q_stored")
        clamp = sem("clamp")
        mT_ps = sem("mT_ps")
        mT_sb = sem("mT_sb")
        mT_split = sem("mT_split")
        m0_split = sem("m0_split")
        ext_in = sem("ext_in")
        ext_flag = sem("ext_flag")
        ext_out = [sem(f"ext_out{g}") for g in range(G)]
        stat_ready = sem("stat_ready")
        stat_ps = sem("stat_ps")
        stat_diag = sem("stat_diag")
        stat_bc = sem("stat_bc")
        flag_ready = sem("flag_ready")
        wq_ready = sem("wq_ready")
        lora_ps = sem("lora_ps")
        lora_sb = sem("lora_sb")
        weff_ps = sem("weff_ps")
        weff_sb = sem("weff_sb")
        v_op_set = sem("v_op_set")
        ctx_loaded = [sem(f"ctx_loaded{p}") for p in range(2)]
        kv_stored = [sem(f"kv_stored{p}") for p in range(2)]
        ctxT_ps = sem("ctxT_ps")
        ctxT_sb = sem("ctxT_sb")
        k_ps = sem("k_ps")
        k_ev = sem("k_ev")
        v_ps = sem("v_ps")
        v_ev = sem("v_ev")
        k_split = sem("k_split")
        kq_loaded = [sem(f"kq_loaded{g}") for g in range(G)]
        v_loaded = sem("v_loaded")
        v_op_ready = sem("v_op_ready")
        s1_ready = sem("s1_ready")
        s1_done = sem("s1_done")
        mx_ready = sem("mx_ready")
        mx_split = sem("mx_split")
        mxT_ps = sem("mxT_ps")
        mxT_sb = sem("mxT_sb")
        s2_ready = sem("s2_ready")
        exp_done = sem("exp_done")
        pv_done = sem("pv_done")
        o_done = sem("o_done")
        o_turned = sem("o_turned")
        inv_ready = sem("inv_ready")
        o_norm = sem("o_norm")
        oT_ps = sem("oT_ps")
        oT_ready = sem("oT_ready")
        y_ps = sem("y_ps")
        mid_ready = sem("mid_ready")
        bo_ready = sem("bo_ready")
        ln2 = sem("ln2")
        var2 = sem("var2")
        rstd2 = sem("rstd2")
        xn2_ready = sem("xn2_ready")
        work_set = sem("work_set")
        stage_ready = sem("stage_ready")
        zeroed = [sem(f"zeroed{g}") for g in range(G)]
        xT2_ps = sem("xT2_ps")
        xT2_sb = sem("xT2_sb")
        h_ps = sem("h_ps")
        h_sb = sem("h_sb")
        out_ps = sem("out_ps")
        out_ready = sem("out_ready")
        out_stored = [sem(f"out_stored{p}") for p in range(2)]

        block = ctx.enter_context(nc.Block())

        TT = (KT + 3) // 4
        CH = cuts(KEYS)

        def chunks_ahead(half):
            def pos(n):
                return CHUNKS * (n + 2 * LEAD) // (2 * KT)
            return range(pos(half), pos(half + 1))

        FIRST = CHUNKS * 2 * LEAD // (2 * KT)

        @block.sync
        def _(sp):
            sp.dma_start(x_sb[:, :, :], io["x"].rearrange("b (t p) d -> p (b t) d", p=P)).then_inc(x_loaded, 16)
            for n, w in enumerate(("Wq", "Wk", "Wv")):
                sp.dma_start(w_qkv[:, n, :], io["L0_xattn_" + w]).then_inc(proj_loaded, 16)
            sp.dma_start(b_qk[:, 0:1], io["L0_xattn_bq"].rearrange("(d a) -> d a", a=1)).then_inc(proj_loaded, 16)
            sp.dma_start(b_qk[:, 1:2], io["L0_xattn_bk"].rearrange("(d a) -> d a", a=1)).then_inc(proj_loaded, 16)
            sp.dma_start(bv_all[:, :], io["L0_xattn_bv"].rearrange("(a d) -> a d", a=1).to_broadcast([P, D])).then_inc(proj_loaded, 16)
            sp.dma_start(mask_q[:, :, :], io["mask_SxS2_fk0"].rearrange("(t p) k -> p t k", p=P)).then_inc(mask_loaded, 16)
            sp.dma_start(mask0[:, :], io["mask_SxS2_fk0"][0:1, :].to_broadcast([P, KEYS])).then_inc(mask_loaded, 16)
            sp.dma_start(w_o[:, :], io["L0_xattn_Wo"]).then_inc(wo_loaded, 16)
            sp.dma_start(bo_all[:, :], io["L0_xattn_bo"].rearrange("(a d) -> a d", a=1).to_broadcast([P, D])).then_inc(wo_loaded, 16)

            sp.wait_ge(m0_split, 1)
            for a in range(PARTS):
                sp.dma_start(ext[PARTS + a:PARTS + a + 1, :], m0_hi[0:1, a * KEYS:(a + 1) * KEYS]).then_inc(ext_in, 16)
            sp.wait_ge(q_split, 3)
            for t in range(TERMS):
                sp.dma_start(q_scr[:, t, :, :].rearrange("h d s -> h d s"), q_bf[:, Q_PART[t], :]).then_inc(q_stored, 16)
            sp.wait_ge(q_stored, 16 * TERMS)
            sp.wait_ge(mT_split, 4)

            def load_ctx(b, p):
                full = (KT - 1) * P
                sp.dma_start(ctx_in[:, p, 0:KT - 1, :],
                             io["ctx_1024"][b, 0:full, :].rearrange("(t p) d -> p t d", p=P)).then_inc(ctx_loaded[p], 16)
                sp.dma_start(ctx_in[0:TAIL, p, KT - 1, :], io["ctx_1024"][b, full:KEYS, :]).then_inc(ctx_loaded[p], 16)

            def store_kv(b, p):
                for a in range(PARTS):
                    sp.dma_start(k_scr[b, :, a, :, :], k_pool[:, p, a, :]).then_inc(kv_stored[p], 16)
                sp.dma_start(v_scr[b, 0:KT - 1, :, :].rearrange("t p d -> p t d"), v_out[:, p, 0:KT - 1, :]).then_inc(kv_stored[p], 16)
                sp.dma_start(v_scr[b, KT - 1, 0:TAIL, :], v_out[0:TAIL, p, KT - 1, :]).then_inc(kv_stored[p], 16)

            sp.wait_ge(q_ps, 4)
            load_ctx(0, 0)
            load_ctx(1, 1)

            def zero_rows(g):
                sp.dma_start(kv_k[KR:P, g, :, :], zeros_src).then_inc(zeroed[g], 16)

            zeros_src = q1_op[KR:P, :, :, :].rearrange("r g h s -> r (g h s)")[:, 0:KEYS].unsqueeze(1).to_broadcast([P - KR, HG, KEYS])
            sp.wait_ge(ext_flag, 1)

            def first_rows(g):
                sp.dma_start(kv_k[0:XR, g, :, :], extf[:, :].unsqueeze(1).to_broadcast([XR, HG, KEYS])).then_inc(ext_out[g], 16)

            for g in range(2):
                zero_rows(g)
                first_rows(g)

            def leave(b, p):
                settled(sp, k_split, b + 1 + 2)
                settled(sp, v_ev, TT * (b + 1) + 2)
                store_kv(b, p)

            with sp.Fori(0, B // 2 - 1) as i:
                for p in range(2):
                    settled(sp, ctxT_ps, TT * (2 * i + p + 1))
                    load_ctx(2 * i + p + 2, p)
                    leave(2 * i + p, p)
            for p in range(2):
                leave(B - 2 + p, p)

            def load_unit(b, g):
                h0 = HG * g
                for r0, np_ in ((0, 3), (3, 2), (5, 1)):
                    sp.dma_start(kv_k[XR + HD * r0:XR + HD * (r0 + np_), g, :, :],
                                 k_scr[b, h0:h0 + HG, 0:np_, :, :].rearrange("h a d k -> (a d) h k")).then_inc(kq_loaded[g], 16)
                src = q_scr[h0:h0 + HG, :, :, bass.ds(b * S, S)].rearrange("h t d s -> (t d) h s")
                sp.dma_start(q1_op[XR:KR, g, :, :], src).then_inc(kq_loaded[g], 16)
                sp.dma_start(q2_op[XR:KR, g, :].rearrange("r (h s) -> r h s", h=HG), src).then_inc(kq_loaded[g], 16)

            def load_v(b):
                sp.dma_start(v_in[:, 0:KT - 1, :], v_scr[b, 0:KT - 1, :, :].rearrange("t p d -> p t d")).then_inc(v_loaded, 16)
                sp.dma_start(v_in[0:TAIL, KT - 1, :], v_scr[b, KT - 1, 0:TAIL, :]).then_inc(v_loaded, 16)

            sp.wait_ge(kv_stored[0], 80 * 2)
            load_unit(0, 0)
            load_unit(0, 1)
            load_v(0)
            for p in range(2):
                sp.wait_ge(kv_stored[p], 80 * (B // 2 + 1))
            for g in range(2, G):
                zero_rows(g)
                first_rows(g)
                load_unit(0, g)
            with sp.Fori(1, B) as i:
                for g in range(G):
                    if g == 2:
                        settled(sp, v_op_ready, G * i)
                        load_v(i)
                    settled(sp, o_done, G * i + g + 1)
                    load_unit(i, g)

            def store_out(b, p):
                sp.dma_start(io["out"][b].rearrange("(t p) d -> p t d", p=P), out_sb[:, p, :, :]).then_inc(out_stored[p], 16)

            with sp.Fori(0, B // 2) as i:
                for p in range(2):
                    settled(sp, out_ready, QT * (2 * i + p + 1))
                    store_out(2 * i + p, p)
            for p in range(2):
                sp.wait_ge(out_stored[p], 16 * (B // 2 + 1))

        @block.gpsimd
        def _(pool):
            n = [0]

            def link(ins):
                n[0] += 1
                ins.then_inc(pool_chain, 1)
                pool.wait_ge(pool_chain, n[0])

            nc.gpsimd.memset(half_neg[:, :], -0.5)
            link(nc.gpsimd.memset(ident[:, :], 0.0))
            link(nc.gpsimd.affine_select(out=ident[:, :], in_=ident[:, :], compare_op=ALU.not_equal, fill=1.0,
                                         base=0, pattern=[[-1, P]], channel_multiplier=1))
            nc.gpsimd.tensor_copy(identb[:, :], ident[:, :]).then_inc(consts, 1)
            link(nc.gpsimd.memset(ones_m[:, :], 0.0))
            nc.gpsimd.memset(ones_m[0:PARTS, :], 1.0).then_inc(consts, 1)
            nc.gpsimd.memset(ones_f[:, :], 1.0).then_inc(consts, 1)
            nc.gpsimd.memset(ext[:, :], 1.0).then_inc(consts, 1)
            nc.gpsimd.memset(q1_op[:, :, :, :], 0.0).then_inc(consts, 1)
            link(nc.gpsimd.memset(q2_op[:, :, :], 0.0))
            nc.gpsimd.memset(q2_op[0:XR, :, :], 1.0).then_inc(consts, 1)
            pool.wait_ge(ln_ready, 1)
            link(nc.gpsimd.tensor_scalar(ln_var[:, :], ln_var[:, :], 1.0 / D, EPS, ALU.mult, ALU.add))
            nc.gpsimd.tensor_tensor(ln_rstd[:, :], ln_var[:, :], half_neg[:, :], ALU.pow).then_inc(rstd_ready, 1)
            for t0, t1 in ((0, KT - 1), (KT - 1, KT)):
                rows = P if t0 == 0 else TAIL
                full = mT_full[0:rows, t0 * S:t1 * S].rearrange("p (t s) -> p t s", s=S)
                res = mT_res[0:rows, t0 * S:t1 * S].rearrange("p (t s) -> p t s", s=S)
                if t0 == 0:
                    pool.wait_ge(mT_sb, KT)
                link(nc.gpsimd.tensor_copy(maskT[0:rows, t0:t1, 0, :], full))
                link(nc.gpsimd.tensor_tensor(res, full, maskT[0:rows, t0:t1, 0, :], ALU.subtract))
                nc.gpsimd.tensor_copy(maskT[0:rows, t0:t1, 1, :], res).then_inc(mT_split, 1)
                pool.wait_ge(mT_split, 1 if t0 == 0 else 3)
                nc.gpsimd.tensor_tensor(maskT[0:rows, t0:t1, 2, :], res, maskT[0:rows, t0:t1, 1, :], ALU.subtract).then_inc(mT_split, 1)
            pool.wait_ge(tanh_ready, 1)
            pool.wait_ge(wo_loaded, 32)
            link(nc.gpsimd.tensor_scalar(bo_all[:, :], bo_all[:, :], tgates[:, 0:1], None, ALU.mult))
            pool.wait_ge(xn_ready, 1)
            nc.gpsimd.tensor_tensor(x_sb[:, :, :], x_sb[:, :, :], bo_all[:, :].unsqueeze(1).to_broadcast([P, B * QT, D]),
                                    ALU.add).then_inc(bo_ready, 1)
            for p in range(2):
                pool.wait_ge(kv_stored[p], 80 * (B // 2 + 1))
            nc.gpsimd.memset(x_all[:, 0:QT, :], 0.0).then_inc(work_set, 1)
            nc.gpsimd.memset(work[:, 0:2 * S + QT * D], 1.0).then_inc(work_set, 1)
            link(nc.gpsimd.memset(v_op[:, :, :, :, :], 0.0))
            nc.gpsimd.memset(v_op[:, :, :, :, HD:HD + 1], 1.0).then_inc(v_op_set, 1)
            pool.wait_ge(v_op_set, 1)

            def spread_v(b, g):
                src = v_in[:, :, HD * HG * g:HD * HG * (g + 1)].rearrange("p t (h d) -> p t h d", h=HG)
                nc.gpsimd.tensor_copy(v_op[:, g, 0:KT - 1, :, 0:HD], src[:, 0:KT - 1])
                nc.gpsimd.tensor_copy(v_op[0:TAIL, g, KT - 1, :, 0:HD], src[0:TAIL, KT - 1]).then_inc(v_op_ready, 1)

            def split_max(u, par):
                settled(pool, mx_ready, u + 1)
                nc.gpsimd.tensor_copy(mx_bf[:, par, :, 0], mx_neg[:, par, :]).then_inc(mx_split, 1)
                pool.wait_ge(mx_split, 4 * u + 1)
                nc.gpsimd.tensor_tensor(mx_res[:, par, :], mx_neg[:, par, :], mx_bf[:, par, :, 0], ALU.subtract).then_inc(mx_split, 1)
                settled(pool, mx_split, 4 * u + 2)
                nc.gpsimd.tensor_copy(mx_bf[:, par, :, 1], mx_res[:, par, :]).then_inc(mx_split, 1)
                pool.wait_ge(mx_split, 4 * u + 3)
                nc.gpsimd.tensor_tensor(mx_bf[:, par, :, 2], mx_res[:, par, :], mx_bf[:, par, :, 1], ALU.subtract).then_inc(mx_split, 1)

            def rstd(n_):
                settled(pool, var2, n_ + 1)
                nc.gpsimd.tensor_scalar(l_var[:, :], l_sum[:, :], 1.0 / D, EPS, ALU.mult, ALU.add).then_inc(rstd2, 1)
                pool.wait_ge(rstd2, 2 * n_ + 1)
                nc.gpsimd.tensor_tensor(l_rstd[:, :], l_var[:, :], half_neg[:, 0:QT], ALU.pow).then_inc(rstd2, 1)

            def unit(i, g, last):
                u = G * i + g
                if g == 1:
                    rstd(i)
                if last and g == G - 1:
                    return
                nxt = G * i + g + 1
                split_max(nxt, (g + 1) % 2)
                if g == G - 1:
                    pool.wait_ge(v_loaded, 32 * (i + 2))
                settled(pool, o_done, nxt + 1)
                spread_v(i + (g + 1) // G, (g + 1) % G)

            split_max(0, 0)
            pool.wait_ge(v_loaded, 32)
            spread_v(0, 0)
            with pool.Fori(0, B - 1) as i:
                for g in range(G):
                    unit(i, g, False)
            for g in range(G):
                unit(B - 1, g, True)

            rstd(B)

        @block.scalar
        def _(act):
            act.dma_start(wf_in.rearrange("p (c d) -> p c d", c=FC), io["L0_ffn_W_fc"].rearrange("(c p) d -> p c d", p=P)).then_inc(ffn_loaded, 16)
            act.dma_start(wp_in, io["L0_ffn_W_proj"]).then_inc(ffn_loaded, 16)
            act.dma_start(gates[:, 0:1], io["g_xattn"].rearrange("(a d) -> a d", a=1).to_broadcast([P, 1])).then_inc(ffn_loaded, 16)
            act.dma_start(gates[:, 1:2], io["g_ffn"].rearrange("(a d) -> a d", a=1).to_broadcast([P, 1])).then_inc(ffn_loaded, 16)
            act.dma_start(a_fc[:, :], io["L0_ffn_A_fc"]).then_inc(ffn_loaded, 16)
            act.dma_start(bl_fc[:, :, :], io["L0_ffn_B_fc"].rearrange("(c p) r -> p c r", p=P)).then_inc(ffn_loaded, 16)
            act.dma_start(a_pj, io["L0_ffn_A_proj"]).then_inc(ffn_loaded, 16)
            act.dma_start(bl_pj[:, :], io["L0_ffn_B_proj"]).then_inc(ffn_loaded, 16)
            act.dma_start(b_fc[:, :], io["L0_ffn_b_fc"].rearrange("(c p) -> p c", p=P),
                          allow_slow_non_contiguous=True).then_inc(ffn_loaded, 16)
            act.dma_start(b_pj[:, :], io["L0_ffn_b_proj"].rearrange("(a d) -> a d", a=1).to_broadcast([P, D])).then_inc(ffn_loaded, 16)
            act.wait_ge(ffn_loaded, 160)
            act.activation(tgates[:, :], gates[:, :], ACT.Tanh).then_inc(tanh_ready, 1)
            act.wait_ge(lora_ps, 1)
            nc.scalar.mul(blT_fc, bank(7)[0:RANK, :], 2.0).then_inc(lora_sb, 1)
            act.wait_ge(lora_ps, 2)
            nc.scalar.mul(blT_pj[:, :], bank(6)[0:RANK, 0:D], 2.0).then_inc(lora_sb, 1)
            for c in range(4):
                act.wait_ge(xnT_ps, c + 1)
                act.activation(xnT[:, c * BANK:(c + 1) * BANK], bank(c), ACT.Copy).then_inc(xnT_sb, 1)
            act.wait_ge(proj_loaded, 96)
            nc.scalar.mul(b_qk[:, 2:3], b_qk[:, 0:1], QSCALE).then_inc(act_chain, 1)
            act.wait_ge(act_chain, 1)
            for c in range(4):
                act.wait_ge(q_ps, c + 1)
                cs = slice(c * BANK, (c + 1) * BANK)
                act.activation(q_full[:, cs], bank(c), ACT.Identity, bias=b_qk[:, 2:3], scale=QSCALE)
                act.activation(q_bf[:, 0, cs], bank(c), ACT.Identity, bias=b_qk[:, 2:3], scale=QSCALE).then_inc(q_ev, 1)
            for t in range(KT):
                r = key_rows(t)
                act.wait_ge(mT_ps, t + 1)
                act.activation(mT_full[0:r, t * S:(t + 1) * S], bank(4 + t % 2)[0:r, 0:S], ACT.Copy).then_inc(mT_sb, 1)
            act.wait_ge(weff_ps, 1)
            act.activation(w_fcT[:, :], bank(6), ACT.Copy).then_inc(weff_sb, 1)
            act.wait_ge(weff_ps, 2)
            act.activation(w_pjT[:, :, :].rearrange("p c d -> p (c d)"), bank(7), ACT.Copy).then_inc(weff_sb, 1)

            act.wait_ge(q_split, 3)
            act.wait_ge(q_stored, 16 * TERMS)
            act.wait_ge(mT_split, 4)
            with act.Fori(0, B // 2) as i:
                for p in range(2):
                    b = 2 * i + p

                    def take_ctx(c):
                        m = TT * b + c
                        lo, hi = CH[c]
                        act.wait_ge(v_ps, m + 1)
                        act.wait_ge(ctxT_ps, m + 1)
                        act.activation(ctxT[:, p, lo:hi], bank(c % 2)[:, 0:hi - lo], ACT.Copy).then_inc(ctxT_sb, 1)

                    def take_k(c):
                        m = TT * b + c
                        lo, hi = CH[c]
                        act.wait_ge(k_ps, m + 1)
                        act.activation(k_full[:, p, lo:hi], bank(2 + c % 2)[:, 0:hi - lo], ACT.Identity, bias=b_qk[:, 1:2])
                        act.activation(k_pool[:, p, 0, lo:hi], bank(2 + c % 2)[:, 0:hi - lo], ACT.Identity, bias=b_qk[:, 1:2]).then_inc(k_ev, 1)

                    act.wait_ge(k_split, b + 1)
                    act.wait_ge(kv_stored[p], 80 * (i + 1))
                    take_ctx(0)
                    for c in range(TT):
                        if c + 1 < TT:
                            take_ctx(c + 1)
                        take_k(c)

            def take_max(u, g):
                act.wait_ge(mxT_ps, u + 1)
                act.activation(q2_op[0:PARTS, g, :], bank(6 + g % 2)[:, :].bitcast(bf16)[0:PARTS, :], ACT.Copy).then_inc(mxT_sb, 1)

            def unit(i, g, last):
                for t in range(KT):
                    step = KT * (G * i + g) + t
                    r = key_rows(t)
                    slot = (KT * g + t) % 4
                    for h in range(2):
                        if h == 0:
                            act.wait_ge(pv_done, step + 1)
                        act.wait_ge(s2_ready, 2 * step + h + 1)
                        act.activation(pt[0:r, slot, h * BANK:(h + 1) * BANK], bank(4 + h)[0:r, :], ACT.Exp).then_inc(exp_done, 1)
                    if t == MX_STEP + 1 and not (last and g == G - 1):
                        take_max(G * i + g + 1, (g + 1) % G)

            take_max(0, 0)
            with act.Fori(0, B - 1) as i:
                for g in range(G):
                    unit(i, g, False)
            for g in range(G):
                unit(B - 1, g, True)

            act.wait_ge(xn2_ready, B + 1)
            with act.Fori(0, B // 2) as i:
                for p in range(2):
                    b = 2 * i + p
                    act.wait_ge(xT2_ps, b + 1)
                    act.activation(x_nT[:, p, :], bank(3)[:, 0:S], ACT.Copy).then_inc(xT2_sb, 1)
                    for c in range(FC):
                        if c % 2 == 0:
                            act.wait_ge(h_ps, FC // 2 * b + c // 2 + 1)
                        act.activation(hT[:, p, c, :], bank(4 + c // 2)[:, (c % 2) * S:(c % 2 + 1) * S], ACT.Gelu,
                                       bias=b_fc[:, c:c + 1]).then_inc(h_sb, 1)

        @block.vector
        def _(dve):
            n = [0]

            def link(ins):
                n[0] += 1
                ins.then_inc(dve_chain, 1)
                dve.wait_ge(dve_chain, n[0])

            for s_, d_ in ((ctxT_sb, 2), (k_ev, 2), (v_ps, 8), (v_ev, 2), (k_split, 2), (pv_done, 4), (o_done, 4),
                           (kv_stored[0], 80), (kv_stored[1], 80), (out_stored[0], 16), (out_stored[1], 16),
                           (o_norm, 1)):
                dve.sem_inc(s_, d_)
            def bc(ap):
                return ap.unsqueeze(2).to_broadcast([P, B * QT, D])
            dve.wait_ge(x_loaded, 16)
            link(nc.vector.reduce_sum(ln_sum[:, :], x_sb[:, :, :], AX.X))
            link(nc.vector.tensor_scalar(ln_mean[:, :], ln_sum[:, :], 1.0 / D, None, ALU.mult))
            link(nc.vector.tensor_tensor(qc[:, :, :], x_sb[:, :, :], bc(ln_mean[:, :]), ALU.subtract))
            link(nc.vector.tensor_tensor(qsq[:, :, :], qc[:, :, :], qc[:, :, :], ALU.mult))
            nc.vector.reduce_sum(ln_var[:, :], qsq[:, :, :], AX.X).then_inc(ln_ready, 1)
            dve.wait_ge(mask_loaded, 32)
            link(nc.vector.tensor_scalar(mask0[:, :], mask0[:, :], -BIG, BIG, ALU.max, ALU.min))
            nc.vector.tensor_scalar(mask_q[:, :, :], mask_q[:, :, :], -BIG, BIG, ALU.max, ALU.min).then_inc(clamp, 1)
            dve.wait_ge(rstd_ready, 1)
            nc.vector.tensor_tensor(qn[:, :, :], qc[:, :, :], bc(ln_rstd[:, :]), ALU.mult).then_inc(xn_ready, 1)
            link(nc.vector.tensor_copy(m0_hi[0:1, 0:KEYS], mask0[0:1, :]))
            link(nc.vector.tensor_tensor(m0_res[0:1, :], mask0[0:1, :], m0_hi[0:1, 0:KEYS], ALU.subtract))
            link(nc.vector.tensor_copy(m0_hi[0:1, KEYS:2 * KEYS], m0_res[0:1, :]))
            nc.vector.tensor_tensor(m0_hi[0:1, 2 * KEYS:3 * KEYS], m0_res[0:1, :], m0_hi[0:1, KEYS:2 * KEYS], ALU.subtract).then_inc(m0_split, 1)
            dve.wait_ge(clamp, 1)
            flat = qsq[:, :, :].rearrange("p t d -> p (t d)")
            for t in range(QT):
                link(nc.vector.tensor_tensor(flat[:, 0:KEYS], mask_q[:, t, :], mask0[:, :], ALU.not_equal))
                link(nc.vector.tensor_reduce(rng[:, t:t + 1], flat[:, 0:KEYS], AX.X, ALU.max))
            link(nc.vector.reduce_max(rng[:, 2:3], mask0[:, :], AX.X))
            link(nc.vector.tensor_scalar(rng[:, 3:4], rng[:, 2:3], PLAIN_TOP, None, ALU.is_gt))
            link(nc.vector.tensor_scalar(rng[:, 2:3], rng[:, 2:3], -PLAIN_TOP, None, ALU.is_lt))
            link(nc.vector.tensor_reduce(stat[:, 2:3], rng[:, :], AX.X, ALU.max))
            dve.wait_ge(ffn_loaded, 160)
            link(nc.vector.tensor_reduce(stat[:, 0:1], wf_in, AX.X, ALU.max, apply_absolute_value=True))
            nc.vector.tensor_reduce(stat[:, 1:2], wp_in, AX.X, ALU.max, apply_absolute_value=True).then_inc(stat_ready, 1)
            dve.wait_ge(stat_ps, 1)
            link(nc.vector.reduce_max(stat_t[:, :], bank(5)[0:PARTS, 0:P], AX.X))
            nc.vector.tensor_scalar(stat_d[:, :], ident[0:PARTS, 0:PARTS], stat_t[:, 0:1], None, ALU.mult).then_inc(stat_diag, 1)
            dve.wait_ge(stat_ps, 2)
            link(nc.vector.tensor_copy(allstat[:, :], bank(5)[:, 0:PARTS]))
            link(nc.vector.tensor_scalar(plain[:, :], allstat[:, 2:3], -1.0, 1.0, ALU.mult, ALU.add))
            nc.vector.tensor_copy(general_i[:, :], allstat[0:1, 2:3]).then_inc(flag_ready, 1)
            link(nc.vector.tensor_scalar(inv_s[:, 0:2], allstat[:, 0:2], 1.0 / QMAX, None, ALU.mult))
            link(nc.vector.reciprocal(inv_s[:, 2:4], inv_s[:, 0:2]))
            for k, (w, r_) in enumerate(((wf_in, wf_r), (wp_in, wp_r))):
                link(nc.vector.tensor_scalar(wf_a, w, inv_s[:, 2 + k:3 + k], MAGIC, ALU.mult, ALU.add))
                link(nc.vector.tensor_scalar(wf_b, wf_a, -MAGIC, -QMAX - 1.0, ALU.add, ALU.max))
                link(nc.vector.tensor_scalar(wf_a, wf_b, QMAX, inv_s[:, k:k + 1], ALU.min, ALU.mult))
                link(nc.vector.tensor_tensor(wf_b, wf_a, w, ALU.subtract))
                nc.vector.tensor_tensor(r_, wf_b, w, ALU.add).then_inc(wq_ready, 1)
                dve.wait_ge(wq_ready, 1 + k)
            dve.wait_ge(q_ev, 4)
            nc.vector.tensor_tensor(q_res[:, :], q_full[:, :], q_bf[:, 0, :], ALU.subtract).then_inc(q_split, 1)
            dve.wait_ge(q_split, 1)
            nc.vector.tensor_copy(q_bf[:, 1, :], q_res[:, :]).then_inc(q_split, 1)
            dve.wait_ge(q_split, 2)
            nc.vector.tensor_tensor(q_bf[:, 2, :], q_res[:, :], q_bf[:, 1, :], ALU.subtract).then_inc(q_split, 1)
            dve.wait_ge(ext_in, 48)
            dve.wait_ge(consts, 6)
            nc.vector.tensor_scalar(extf[:, :], ext[:, :], plain[0:XR, 0:1], None, ALU.mult).then_inc(ext_flag, 1)

            dve.wait_ge(q_stored, 16 * TERMS)
            dve.wait_ge(mT_split, 4)
            dve.wait_ge(q_ps, 4)
            ksub = sem("ksub")
            with dve.Fori(0, B // 2) as i:
                for p in range(2):
                    b = 2 * i + p
                    dve.wait_ge(kv_stored[p], 80 * (i + 1))
                    for c in range(TT):
                        dve.wait_ge(v_ps, TT * b + c + 1 + 8)
                        tiles = min(4, KT - 4 * c)
                        rows = P if tiles == 4 else TAIL
                        nc.vector.tensor_tensor(v_out[0:rows, p, 4 * c:4 * c + tiles, :],
                                                bank(4 + c % 2)[0:rows, 0:tiles * D].rearrange("p (t d) -> p t d", d=D),
                                                bv_all[0:rows, :].unsqueeze(1).to_broadcast([rows, tiles, D]),
                                                ALU.add).then_inc(v_ev, 1)
                    dve.wait_ge(k_ev, TT * (b + 1) + 2)
                    nc.vector.tensor_tensor(k_res[:, :], k_full[:, p, :], k_pool[:, p, 0, :], ALU.subtract).then_inc(ksub, 1)
                    dve.wait_ge(ksub, 2 * b + 1)
                    nc.vector.tensor_copy(k_pool[:, p, 1, :], k_res[:, :]).then_inc(ksub, 1)
                    dve.wait_ge(ksub, 2 * b + 2)
                    nc.vector.tensor_tensor(k_pool[:, p, 2, :], k_res[:, :], k_pool[:, p, 1, :], ALU.subtract).then_inc(k_split, 1)

            def chunk(i, g, c):
                u = G * i + g
                qh, half = c // 2, c % 2
                lo = half * HALF
                width = min(HALF, KEYS - lo)
                pos = CHUNKS * u + c
                two = ps[:, 2 * half:2 * half + 2, :].rearrange("p a n -> p (a n)")
                settled(dve, s1_ready, pos + 1)
                nc.vector.tensor_tensor_reduce(out=two[:, 0:width], in0=two[:, 0:width],
                                               in1=mask_q[:, qh % QT, lo:lo + width], scale=1.0, scalar=-3.4e38,
                                               op0=ALU.add, op1=ALU.max,
                                               accum_out=mx_part[:, g % 2, qh, half:half + 1]).then_inc(s1_done, 1)
                if c == CHUNKS - 1:
                    dve.wait_ge(s1_done, pos + 1)
                    nc.vector.tensor_reduce(mx_neg[:, g % 2, :], mx_part[:, g % 2, :, :], AX.X, ALU.max,
                                            negate=True).then_inc(mx_ready, 1)

            def normalise(u, slot):
                turned = bank(6 + slot % 2)[:, S:2 * S].rearrange("p (t j r) -> p t j r", t=QT, j=HG)
                dve.wait_ge(o_norm, u + 1)
                settled(dve, o_turned, u + 1)
                nc.vector.reciprocal(o_inv[:, :, :], turned[:, :, :, HD]).then_inc(inv_ready, 1)
                dve.wait_ge(inv_ready, u + 1)
                nc.vector.tensor_tensor(o_q[:, :, HG * HD * slot:HG * HD * (slot + 1)].rearrange("p t (j d) -> p t j d", j=HG),
                                        turned[:, :, :, 0:HD], o_inv[:, :, :].unsqueeze(3).to_broadcast([P, QT, HG, HD]),
                                        ALU.mult).then_inc(o_norm, 1)

            def take_oT(n_):
                dve.wait_ge(oT_ps, n_ + 1)
                nc.vector.tensor_copy(oT, bank(7)[:, 0:S]).then_inc(oT_ready, 1)

            def tiles(ap, n_):
                return ap[:, QT * n_:QT * (n_ + 1), :] if isinstance(n_, int) else ap[:, bass.ds(QT * n_, QT), :]

            def take_y(n_):
                dve.wait_ge(y_ps, n_ + 1)
                nc.vector.scalar_tensor_tensor(out=tiles(x_all, n_), in0=bank(7)[:, S:S + QT * D].rearrange("p (t d) -> p t d", t=QT),
                                               scalar=tgates[:, 0:1], in1=tiles(x_all, n_),
                                               op0=ALU.mult, op1=ALU.add).then_inc(mid_ready, 1)

            def norm_step(n_, k):
                xm = tiles(x_all, n_)
                if k == 0:
                    settled(dve, mid_ready, n_ + 1)
                    nc.vector.reduce_sum(l_mean[:, :], xm, AX.X).then_inc(ln2, 1)
                elif k == 1:
                    dve.wait_ge(ln2, 4 * n_ + 1)
                    nc.vector.tensor_scalar(l_mean[:, :], l_mean[:, :], 1.0 / D, None, ALU.mult).then_inc(ln2, 1)
                elif k == 2:
                    dve.wait_ge(ln2, 4 * n_ + 2)
                    nc.vector.tensor_tensor(x_c, xm, l_mean[:, :].unsqueeze(2).to_broadcast([P, QT, D]), ALU.subtract).then_inc(ln2, 1)
                elif k == 3:
                    dve.wait_ge(ln2, 4 * n_ + 3)
                    nc.vector.tensor_tensor(x_q, x_c, x_c, ALU.mult).then_inc(ln2, 1)
                elif k == 4:
                    dve.wait_ge(ln2, 4 * n_ + 4)
                    nc.vector.reduce_sum(l_sum[:, :], x_q, AX.X).then_inc(var2, 1)
                else:
                    dve.wait_ge(rstd2, 2 * n_ + 2)
                    nc.vector.tensor_tensor(tiles(x_n, n_), x_c, l_rstd[:, :].unsqueeze(2).to_broadcast([P, QT, D]),
                                            ALU.mult).then_inc(xn2_ready, 1)

            def unit(i, g, last):
                u = G * i + g
                for t in range(KT):
                    for c in [*chunks_ahead(2 * t), *chunks_ahead(2 * t + 1)]:
                        ahead = g + 1 + c // CHUNKS
                        if not (last and ahead >= G):
                            chunk(i, ahead, c % CHUNKS)
                    if t == O_STEP + 1:
                        normalise(u, (g - 1) % G)
                    if g == 0 and t == OT_STEP + 1:
                        take_oT(i)
                    if g == 0 and t == Y_STEP + 1:
                        take_y(i)
                    if g == 1 and t in LN_STEPS:
                        norm_step(i, LN_STEPS.index(t))
                dve.wait_ge(pv_done, KT * (u + 1) + 4)
                nc.vector.tensor_copy(o_raw[:, g % 2, :], bank(6 + g % 2)[:, 0:S]).then_inc(o_done, 1)

            for c in range(CHUNKS):
                chunk(0, 0, c)
            for c in range(FIRST):
                chunk(0, 1, c)
            with dve.Fori(0, B - 1) as i:
                for g in range(G):
                    unit(i, g, False)
            for g in range(G):
                unit(B - 1, g, True)

            normalise(B * G, G - 1)
            take_oT(B)
            take_y(B)
            for k in range(len(LN_STEPS)):
                norm_step(B, k)

            e2 = sem("e2")

            def stage(b, p):
                nc.vector.tensor_copy(x_nS[:, p, :, :], tiles(x_n, b + 1)).then_inc(stage_ready, 1)
                nc.vector.scalar_tensor_tensor(out=x_res[:, p, :, :],
                                               in0=b_pj[:, :].unsqueeze(1).to_broadcast([P, QT, D]),
                                               scalar=tgates[:, 1:2], in1=tiles(x_all, b + 1),
                                               op0=ALU.mult, op1=ALU.add).then_inc(e2, 1)

            def finish(b, p, i):
                dve.wait_ge(e2, b + 1)
                dve.wait_ge(out_stored[p], 16 * (i + 1))
                for t in range(QT):
                    dve.wait_ge(out_ps, QT * b + t + 1)
                    nc.vector.scalar_tensor_tensor(out=out_sb[:, p, t, :], in0=bank(6 + t)[:, 0:D],
                                                   scalar=tgates[:, 1:2], in1=x_res[:, p, t, :],
                                                   op0=ALU.mult, op1=ALU.add).then_inc(out_ready, 1)

            with dve.Fori(0, B // 2) as i:
                for p in range(2):
                    stage(2 * i + p, p)
                    finish(2 * i + p, p, i)

        @block.tensor
        def _(pe):
            pe.wait_ge(consts, 6)
            pe.wait_ge(ffn_loaded, 160)
            for c in range(FC):
                m = nc.tensor.transpose(bank(7)[0:RANK, c * P:(c + 1) * P], bl_fc[:, c, :], ident[:, :])
            m.then_inc(lora_ps, 1)
            nc.tensor.transpose(bank(6)[0:RANK, 0:P], bl_pj[:, :], ident[:, :]).then_inc(lora_ps, 1)
            pe.wait_ge(xn_ready, 1)
            for c in range(4):
                for k in range(4):
                    m = nc.tensor.transpose(bank(c)[:, k * P:(k + 1) * P], qn[:, 4 * c + k, :], ident[:, :])
                m.then_inc(xnT_ps, 1)
            pe.wait_ge(proj_loaded, 96)
            for c in range(4):
                pe.wait_ge(xnT_sb, c + 1)
                nc.tensor.matmul(bank(c), w_qkv[:, 0, :], xnT[:, c * BANK:(c + 1) * BANK], start=True, stop=True).then_inc(q_ps, 1)
            pe.wait_ge(clamp, 1)
            for t in range(KT):
                r = key_rows(t)
                if t >= 2:
                    pe.wait_ge(mT_sb, t - 1)
                for k in range(QT):
                    m = nc.tensor.transpose(bank(4 + t % 2)[0:r, k * P:(k + 1) * P], mask_q[:, k, t * P:t * P + r], ident[:, :])
                m.then_inc(mT_ps, 1)
            pe.wait_ge(stat_ready, 1)
            pe.wait_ge(mT_sb, KT)
            nc.tensor.transpose(bank(5)[0:PARTS, 0:P], stat[:, :], ident[:, :]).then_inc(stat_ps, 1)
            pe.wait_ge(stat_diag, 1)
            nc.tensor.matmul(bank(5)[:, 0:PARTS], ones_f[:, :], stat_d[:, :], start=True, stop=True).then_inc(stat_ps, 1)
            pe.wait_ge(lora_sb, 2)
            pe.wait_ge(wq_ready, 1)
            for c in range(FC):
                cs = slice(c * P, (c + 1) * P)
                nc.tensor.matmul(bank(6)[:, cs], wf_r[:, cs], ident[:, :], start=True, stop=False)
                m = nc.tensor.matmul(bank(6)[:, cs], a_fc[:, :], blT_fc[:, cs], start=False, stop=True)
            m.then_inc(weff_ps, 1)
            pe.wait_ge(wq_ready, 2)
            for c in range(FC):
                cs = slice(c * P, (c + 1) * P)
                nc.tensor.matmul(bank(7)[:, cs], wp_r[:, cs], ident[:, :], start=True, stop=False)
                m = nc.tensor.matmul(bank(7)[:, cs], a_pj[:, cs], blT_pj[:, :], start=False, stop=True)
            m.then_inc(weff_ps, 1)

            pe.wait_ge(q_ev, 4)
            pe.wait_ge(stat_ps, 2)
            pe.wait_ge(flag_ready, 1)
            with pe.Fori(0, B // 2) as i:
                for p in range(2):
                    b = 2 * i + p

                    def turn(c):
                        pe.wait_ge(ctxT_sb, TT * b + c + 1)
                        for t in range(4 * c, min(4 * c + 4, KT)):
                            r = key_rows(t)
                            m = nc.tensor.transpose(bank(c % 2)[:, (t % 4) * P:(t % 4) * P + r], ctx_in[0:r, p, t, :], ident[0:r, 0:r])
                        m.then_inc(ctxT_ps, 1)

                    def project(c):
                        n_ = TT * b + c
                        lo, hi = CH[c]
                        pe.wait_ge(ctxT_sb, n_ + 1 + 2)
                        pe.wait_ge(k_ev, n_ + 1)
                        nc.tensor.matmul(bank(2 + c % 2)[:, 0:hi - lo], w_qkv[:, 1, :], ctxT[:, p, lo:hi],
                                         start=True, stop=True).then_inc(k_ps, 1)
                        pe.wait_ge(v_ev, n_ + 1)
                        for t in range(4 * c, min(4 * c + 4, KT)):
                            r = key_rows(t)
                            m = nc.tensor.matmul(bank(4 + c % 2)[0:r, (t % 4) * D:(t % 4 + 1) * D],
                                                 ctxT[:, p, t * P:t * P + r], w_qkv[:, 2, :], start=True, stop=True)
                        m.then_inc(v_ps, 1)

                    pe.wait_ge(ctx_loaded[p], 32 * (i + 1))
                    turn(0)
                    for c in range(TT):
                        if c + 1 < TT:
                            turn(c + 1)
                        project(c)

            general = pe.value_load(general_i[0:1, 0:1], min_val=0, max_val=1)

            def chunk(i, g, c):
                u = G * i + g
                slot = g % G
                qh, half = c // 2, c % 2
                h, qt = qh // QT, qh % QT
                lo = half * HALF
                width = min(HALF, KEYS - lo)
                pos = CHUNKS * u + c
                if c == 0:
                    pe.wait_ge(kq_loaded[slot], 80 * (i + g // G + 1))
                    pe.wait_ge(ext_out[slot], 16)
                    pe.wait_ge(zeroed[slot], 16)
                if not (isinstance(i, int) and pos < 2):
                    pe.wait_ge(s1_done, pos - 1)
                for k, (a, z) in enumerate(cuts(width)):
                    m = nc.tensor.matmul(ps[:, 2 * half + k, 0:z - a], q1_op[:, slot, h, qt * P:(qt + 1) * P],
                                         kv_k[:, slot, h, lo + a:lo + z], start=True, stop=True)
                m.then_inc(s1_ready, 1)

            def turn_max(u, slot, batch):
                pe.wait_ge(mx_split, 4 * (u + 1))
                pe.wait_ge(o_norm, u + 1)
                if slot == 1:
                    pe.wait_ge(mid_ready, batch + 1)
                rows = bank(6 + slot % 2)[:, :].bitcast(bf16)
                for j in range(HG * QT):
                    m = nc.tensor.transpose(rows[0:PARTS, j * P:(j + 1) * P], mx_bf[:, slot % 2, j, :], identb[:, :])
                m.then_inc(mxT_ps, 1)

            def sweep2(i, g, t, arm):
                slot = g % G
                step = KT * (G * i + g) + t
                r = key_rows(t)
                if t == 0:
                    pe.wait_ge(mxT_sb, G * i + g + 1)
                for k in range(2):
                    if not (isinstance(i, int) and step == 0):
                        pe.wait_ge(exp_done, 2 * step + k - 1)
                    out = bank(4 + k)[0:r, :]
                    if arm == "general":
                        for a in range(PARTS):
                            nc.tensor.matmul(out.rearrange("p (h s) -> p h s", h=2), identb[0:r, 0:r],
                                             maskT[0:r, t, a, :].unsqueeze(1).to_broadcast([r, 2, S]),
                                             start=(a == 0), stop=False)
                    for h in range(2 * k, 2 * k + 2):
                        m = nc.tensor.matmul(out[:, (h % 2) * S:(h % 2 + 1) * S], kv_k[:, slot, h, t * P:t * P + r],
                                             q2_op[:, slot, h * S:(h + 1) * S],
                                             start=(arm != "general"), stop=(arm != "general"))
                    if arm == "general":
                        m = nc.tensor.matmul(out, ones_m[:, 0:r], q2_op[:, slot, 2 * k * S:(2 * k + 2) * S],
                                             start=False, stop=True)
                    m.then_inc(s2_ready, 1)

            def multiply_v(i, g, t):
                step = KT * (G * i + g) + t
                r = key_rows(t)
                if t == 0:
                    pe.wait_ge(v_op_ready, G * i + g + 1)
                pe.wait_ge(exp_done, 2 * step + 2)
                for h in range(HG):
                    m = nc.tensor.matmul(bank(6 + g % 2)[32 * h:32 * h + 32, 0:S], v_op[0:r, g, t, h, :],
                                         pt[0:r, (KT * g + t) % 4, h * S:(h + 1) * S],
                                         start=(t == 0), stop=(t == KT - 1))
                m.then_inc(pv_done, 1)

            def turn_o(u, par):
                pe.wait_ge(o_done, u + 4)
                for t in range(QT):
                    m = nc.tensor.transpose(bank(6 + par)[:, S + t * P:S + (t + 1) * P], o_raw[:, par, t * P:(t + 1) * P], ident[:, :])
                m.then_inc(o_turned, 1)

            def turn_back(n_):
                pe.wait_ge(o_norm, G * n_ + 1 + 1)
                for t in range(QT):
                    m = nc.tensor.transpose(bank(7)[:, t * P:(t + 1) * P], o_q[:, t, :], ident[:, :])
                m.then_inc(oT_ps, 1)

            def project_o(n_):
                pe.wait_ge(oT_ready, n_ + 1)
                for t in range(QT):
                    m = nc.tensor.matmul(bank(7)[:, S + t * D:S + (t + 1) * D], oT[:, t * P:(t + 1) * P], w_o[:, :],
                                         start=True, stop=True)
                m.then_inc(y_ps, 1)

            def unit(i, g, last, arm):
                def ahead(half):
                    for c in chunks_ahead(half):
                        unit_ = g + 1 + c // CHUNKS
                        if not (last and unit_ >= G):
                            chunk(i, unit_, c % CHUNKS)

                for t in range(KT):
                    final = last and g == G - 1
                    ahead(2 * t)
                    if t + 1 < KT:
                        sweep2(i, g, t + 1, arm)
                    elif not final:
                        sweep2(i, g + 1, 0, arm)
                    if t == O_STEP:
                        turn_o(G * i + g, (g - 1) % 2)
                    if g == 0 and t == OT_STEP:
                        turn_back(i)
                    if g == 0 and t == Y_STEP:
                        project_o(i)
                    if t == MX_STEP and not final:
                        turn_max(G * i + g + 1, (g + 1) % G, i)
                    ahead(2 * t + 1)
                    multiply_v(i, g, t)

            def either(body):
                with pe.If(general != 0):
                    body("general")
                with pe.Else():
                    body("plain")

            pe.wait_ge(wo_loaded, 32)
            pe.wait_ge(work_set, 2)
            for c in range(CHUNKS):
                chunk(0, 0, c)
            for c in range(FIRST):
                chunk(0, 1, c)
            turn_max(0, 0, 0)
            either(lambda arm: sweep2(0, 0, 0, arm))
            with pe.Fori(0, B - 1) as i:
                either(lambda arm: [unit(i, g, False, arm) for g in range(G)])
            either(lambda arm: [unit(B - 1, g, True, arm) for g in range(G)])

            turn_o(B * G, 1)
            turn_back(B)
            project_o(B)

            def ffn(b, p):
                pe.wait_ge(stage_ready, b + 1)
                for t in range(QT):
                    m = nc.tensor.transpose(bank(3)[:, t * P:(t + 1) * P], x_nS[:, p, t, :], ident[:, :])
                m.then_inc(xT2_ps, 1)
                pe.wait_ge(xT2_sb, b + 1)
                for c in range(FC):
                    m = nc.tensor.matmul(bank(4 + c // 2)[:, (c % 2) * S:(c % 2 + 1) * S], w_fcT[:, c * P:(c + 1) * P],
                                         x_nT[:, p, :], start=True, stop=True)
                    if c % 2:
                        m.then_inc(h_ps, 1)
                for t in range(QT):
                    for c in range(FC):
                        pe.wait_ge(h_sb, FC * b + c + 1)
                        m = nc.tensor.matmul(bank(6 + t)[:, 0:D], hT[:, p, c, t * P:(t + 1) * P], w_pjT[:, c, :],
                                             start=(c == 0), stop=(c == FC - 1))
                    m.then_inc(out_ps, 1)

            with pe.Fori(0, B // 2) as i:
                for p in range(2):
                    ffn(2 * i + p, p)


_INS = ['x', 'ctx_1024', 'mask_SxS2_fk0', 'g_xattn', 'g_ffn', 'L0_xattn_Wq', 'L0_xattn_bq', 'L0_xattn_Wk', 'L0_xattn_bk',
        'L0_xattn_Wv', 'L0_xattn_bv', 'L0_xattn_Wo', 'L0_xattn_bo', 'L0_ffn_W_fc', 'L0_ffn_b_fc', 'L0_ffn_A_fc',
        'L0_ffn_B_fc', 'L0_ffn_W_proj', 'L0_ffn_b_proj', 'L0_ffn_A_proj', 'L0_ffn_B_proj']


def kernel(**inputs):
    import numpy as _np
    import concourse.bacc as _bacc
    from concourse import mybir as _mybir
    from concourse.bass_utils import run_bass_kernel_spmd as _run

    nc = _bacc.Bacc("TRN2", target_bir_lowering=False, num_devices=1)
    arrays, io = {}, {}
    for name in _INS:
        a = _np.ascontiguousarray(inputs[name])
        arrays[f"in_{name}"] = a
        io[name] = nc.dram_tensor(f"in_{name}", a.shape, _mybir.dt.from_np(a.dtype), kind="ExternalInput").ap()
    shape = arrays["in_x"].shape
    io["out"] = nc.dram_tensor("out_0", shape, _mybir.dt.float32, kind="ExternalOutput").ap()
    flamingo_block(nc, io)
    r = _run(nc, [arrays], core_ids=[0])
    return r.results[0]["out_0"]
```

```python
import concourse.bass as bass
from concourse import mybir
from contextlib import ExitStack


def flamingo_block(nc, io):
    fp32, bf16, i32 = mybir.dt.float32, mybir.dt.bfloat16, mybir.dt.int32
    ALU = mybir.AluOpType
    ACT = mybir.ActivationFunctionType
    AX = mybir.AxisListType

    B, S, D = io["x"].shape
    KEYS = io["ctx_1024"].shape[1]
    F = io["L0_ffn_W_fc"].shape[0]
    RANK = io["L0_ffn_A_fc"].shape[0]
    P = 128
    NH, HD = 16, D // 16
    HG = 4
    G = NH // HG
    QT = S // P
    KT = -(-KEYS // P)
    TAIL = KEYS - (KT - 1) * P
    BANK = 512
    HALF = (KEYS + 1) // 2
    PARTS = 3
    K_PART = [0, 1, 2, 0, 1, 0]
    Q_PART = [0, 0, 0, 1, 1, 2]
    FIRST_TERM = [0, 3, 5]
    TERMS = len(K_PART)
    TR = TERMS * HD
    XR = 2 * PARTS
    KR = XR + TR
    FC = F // P
    TOK = B * S
    QSCALE = float(HD) ** -0.5
    BIG = 3.0e38
    PLAIN_TOP = 1024.0
    EPS = 1e-5
    QMAX = 127.0
    MAGIC = 1.5 * 2.0 ** 23
    CHUNKS = 2 * QT * HG
    LEAD = 5
    O_STEP, OT_STEP, Y_STEP = 2, 5, 7
    LN_STEPS = ((1, 0), (1, 9), (1, 10), (1, 11), (2, 0), (2, 10))
    PREPARE = 9
    MX_STEP = 10

    def key_rows(t):
        return P if t < KT - 1 else TAIL

    def settled(eng, sem_, value):
        eng.wait_ge(sem_, value)
        eng.sem_inc(passed, 1)

    def cuts(width):
        return [(a, min(a + BANK, width)) for a in range(0, width, BANK)]

    with ExitStack() as ctx:
        def sb(name, shape, dt):
            return ctx.enter_context(nc.sbuf_tensor(name, shape, dt))

        def sem(name):
            return ctx.enter_context(nc.semaphore(name))

        ps = ctx.enter_context(nc.psum_tensor("ps", [P, 8, BANK], fp32))

        def bank(n):
            return ps[:, n, :]

        k_op = sb("k_op", [P, G * HG * KEYS], bf16)
        q_ops = sb("q_ops", [P, 2, G * HG * S], bf16)
        q1_op = q_ops[:, 0, :].rearrange("p (g h s) -> p g h s", g=G, h=HG)
        q2_op = q_ops[:, 1, :].rearrange("p (g s) -> p g s", g=G)
        v_in = sb("v_in", [P, KT, D], fp32)
        v_op = sb("v_op", [P, G, KT, HG, 32], fp32)
        mask_q = sb("mask_q", [P, QT, KEYS], fp32)
        maskT = sb("maskT", [P, KT, PARTS, S], bf16)
        x_all = sb("x_all", [P, QT + B * QT, D], fp32)
        x_sb = x_all[:, QT:, :]
        work = sb("work", [P, B * G * S], fp32)
        pt = sb("pt", [P, 4, HG * S], fp32)
        ext_sb = sb("ext_sb", [XR, KEYS], bf16)
        w_qkv = sb("w_qkv", [P, 3, D], fp32)
        b_qk = sb("b_qk", [P, 3], fp32)
        bv_col = sb("bv_col", [P, 1], fp32)
        w_o = sb("w_o", [P, D], fp32)
        bo_all = sb("bo_all", [P, D], fp32)
        ident = sb("ident", [P, P], fp32)
        identb = sb("identb", [P, P], bf16)
        ones_m = sb("ones_m", [P, P], bf16)
        ones_f = sb("ones_f", [PARTS, P], fp32)
        gates = sb("gates", [P, 2], fp32)
        tgates = sb("tgates", [P, 2], fp32)
        stat = sb("stat", [P, 2], fp32)
        stat_m = sb("stat_m", [P, 1], fp32)
        flag_t = sb("flag_t", [1, 1], fp32)
        rng = sb("rng", [P, 4], fp32)
        stat_t = sb("stat_t", [2, 1], fp32)
        stat_d = sb("stat_d", [2, 2], fp32)
        allstat = sb("allstat", [P, 2], fp32)
        plain = sb("plain", [P, 1], fp32)
        general_i = sb("general_i", [1, 1], i32)
        half_neg = sb("half_neg", [P, B * QT], fp32)
        ln_sum = sb("ln_sum", [P, B * QT], fp32)
        ln_mean = sb("ln_mean", [P, B * QT], fp32)
        ln_var = sb("ln_var", [P, B * QT], fp32)
        ln_rstd = sb("ln_rstd", [P, B * QT], fp32)
        mx_part = sb("mx_part", [P, 2, HG * QT, 2], fp32)
        mx_neg = sb("mx_neg", [P, 2, HG * QT], fp32)
        mx_res = sb("mx_res", [P, 2, HG * QT], fp32)
        mx_bf = sb("mx_bf", [P, 2, HG * QT, PARTS], bf16)
        w_fcT = sb("w_fcT", [P, F], fp32)
        w_pjT = sb("w_pjT", [P, FC, D], fp32)
        b_fc = sb("b_fc", [P, FC], fp32)
        b_pj = sb("b_pj", [P, D], fp32)
        l_sum = sb("l_sum", [P, QT], fp32)
        l_mean = sb("l_mean", [P, QT], fp32)
        l_var = sb("l_var", [P, QT], fp32)
        l_rstd = sb("l_rstd", [P, QT], fp32)

        kv_k = k_op[:, :].rearrange("p (g h k) -> p g h k", g=G, h=HG)
        off = 2 * HG * KEYS
        k_pool = k_op[:, off:off + 2 * PARTS * KEYS].rearrange("p (b a k) -> p b a k", b=2, a=PARTS)
        v_flat = v_op[:, :, :, :, :].rearrange("p g t h c -> p (g t h c)")
        v_out = v_flat[:, 0:2 * KT * D].rearrange("p (b t d) -> p b t d", b=2, t=KT)
        k_res = v_flat[:, 2 * KT * D:2 * KT * D + KEYS]
        work_flat = work[:, :]
        ctx_in = work_flat[:, 0:2 * KT * D].rearrange("p (b t d) -> p b t d", b=2, t=KT)
        ctxT = work_flat[:, 2 * KT * D:2 * KT * D + 2 * KEYS].rearrange("p (b k) -> p b k", b=2)
        pt_flat = pt[:, :, :].rearrange("p n s -> p (n s)")
        k_full = pt_flat[:, 0:2 * KEYS].rearrange("p (b k) -> p b k", b=2)
        qn = pt_flat[:, 0:TOK].rearrange("p (t d) -> p t d", d=D)
        qsq = pt_flat[:, TOK:2 * TOK].rearrange("p (t d) -> p t d", d=D)
        xnT = work_flat[:, 2 * KT * D:2 * KT * D + TOK]
        q_bf = k_op[:, 0:PARTS * TOK].rearrange("p (a s) -> p a s", a=PARTS)
        q_full = k_op[:, PARTS * TOK:(PARTS + 2) * TOK].bitcast(fp32)
        mT_full = q_ops[:, :, :].rearrange("p a s -> p (a s)")[:, 0:2 * KT * S].bitcast(fp32)
        mask0 = v_in[:, :, :].rearrange("p t d -> p (t d)")[:, 0:KEYS]
        m0_off = off + PARTS * KEYS
        m0_parts = k_op[:, m0_off:m0_off + PARTS * KEYS]
        differ1 = work_flat[:, 2 * KT * D + 2 * KEYS:2 * KT * D + 3 * KEYS]
        m0_res = k_op[:, off:off + 2 * KEYS].bitcast(fp32)
        differ0 = v_flat[:, 2 * KT * D + KEYS:2 * KT * D + 2 * KEYS]
        slots = k_op[:, :].bitcast(fp32).rearrange("p (g k) -> p g k", g=G)
        out_sb = v_flat[:, 0:2 * QT * D].rearrange("p (b t d) -> p b t d", b=2, t=QT)
        x_nT = v_flat[:, 2 * QT * D:4 * QT * D].rearrange("p (b s) -> p b s", b=2)
        x_nS = v_flat[:, 4 * QT * D:6 * QT * D].rearrange("p (b t d) -> p b t d", b=2, t=QT)
        hT = pt_flat[:, 0:2 * FC * S].rearrange("p (b c s) -> p b c s", b=2, c=FC)
        o_raw = work[:, 0:2 * S].rearrange("p (b s) -> p b s", b=2)
        o_q = work[:, 2 * S:2 * S + QT * D].rearrange("p (t d) -> p t d", t=QT)
        w0 = 2 * S + QT * D
        oT = work[:, w0:w0 + S]
        w0 = w0 + S
        x_c = work[:, w0:w0 + QT * D].rearrange("p (t d) -> p t d", t=QT)
        x_q = work[:, w0 + QT * D:w0 + 2 * QT * D].rearrange("p (t d) -> p t d", t=QT)
        w1 = w0 + 2 * QT * D
        x_n = work[:, w1:w1 + (1 + B) * QT * D].rearrange("p (t d) -> p t d", d=D)

        f0 = w1 + (1 + B) * QT * D
        wf_in, wp_in, wf_a, wf_b, wf_r, wp_r = (work[:, f0 + k * F:f0 + (k + 1) * F] for k in range(6))
        a_pj = work[0:RANK, f0 + 6 * F:f0 + 7 * F]
        blT_fc = work[0:RANK, f0 + 7 * F:f0 + 8 * F]
        blT_pj = sb("blT_pj", [RANK, D], fp32)
        o_inv = sb("o_inv", [P, QT, HG], fp32)
        inv_s = sb("inv_s", [P, 4], fp32)
        a_fc = sb("a_fc", [RANK, D], fp32)
        bl_fc = sb("bl_fc", [P, FC, RANK], fp32)
        bl_pj = sb("bl_pj", [P, RANK], fp32)

        k_scr = nc.dram_tensor("k_scr", [B, NH, PARTS, HD, KEYS], bf16, kind="Internal").ap()
        q_scr = nc.dram_tensor("q_scr", [NH, TERMS, HD, B * S], bf16, kind="Internal").ap()
        v_scr = nc.dram_tensor("v_scr", [B, KT, P, D], fp32, kind="Internal").ap()

        passed = sem("passed")
        x_loaded = sem("x_loaded")
        proj_loaded = sem("proj_loaded")
        mask_loaded = sem("mask_loaded")
        ffn_loaded = sem("ffn_loaded")
        wo_loaded = sem("wo_loaded")
        consts = sem("consts")
        pool_chain = sem("pool_chain")
        dve_chain = sem("dve_chain")
        act_chain = sem("act_chain")
        tanh_ready = sem("tanh_ready")
        ln_ready = sem("ln_ready")
        rstd_ready = sem("rstd_ready")
        xn_ready = sem("xn_ready")
        xnT_ps = sem("xnT_ps")
        xnT_sb = sem("xnT_sb")
        q_ps = sem("q_ps")
        q_ev = sem("q_ev")
        q_split = sem("q_split")
        q_stored = sem("q_stored")
        q_repeated = sem("q_repeated")
        mask_clamped = sem("mask_clamped")
        mT_hi = sem("mT_hi")
        mT_mid = sem("mT_mid")
        differ_ready = sem("differ_ready")
        q_ops_set = sem("q_ops_set")
        slot_set = sem("slot_set")
        mT_ps = sem("mT_ps")
        mT_sb = sem("mT_sb")
        mT_split = sem("mT_split")
        m0_split = sem("m0_split")
        ext_in = sem("ext_in")
        ext_flag = sem("ext_flag")
        ext_out = [sem(f"ext_out{g}") for g in range(G)]
        flag_part = sem("flag_part")
        flag_ps = sem("flag_ps")
        flag_row = sem("flag_row")
        weights_loaded = sem("weights_loaded")
        x_out = sem("x_out")
        stat_ready = sem("stat_ready")
        stat_ps = sem("stat_ps")
        stat_diag = sem("stat_diag")
        flag_ready = sem("flag_ready")
        wq_ready = sem("wq_ready")
        lora_ps = sem("lora_ps")
        lora_sb = sem("lora_sb")
        weff_ps = sem("weff_ps")
        weff_sb = sem("weff_sb")
        v_op_set = sem("v_op_set")
        ctx_loaded = [sem(f"ctx_loaded{p}") for p in range(2)]
        k_stored = [sem(f"k_stored{p}") for p in range(2)]
        v_stored = [sem(f"v_stored{p}") for p in range(2)]
        ctxT_ps = sem("ctxT_ps")
        ctxT_sb = sem("ctxT_sb")
        k_ps = sem("k_ps")
        k_ev = sem("k_ev")
        v_ps = sem("v_ps")
        v_ev = sem("v_ev")
        k_split = sem("k_split")
        kq_loaded = [sem(f"kq_loaded{g}") for g in range(G)]
        v_loaded = sem("v_loaded")
        v_op_ready = sem("v_op_ready")
        s1_ready = sem("s1_ready")
        s1_done = sem("s1_done")
        mx_ready = sem("mx_ready")
        mx_split = sem("mx_split")
        mxT_ps = sem("mxT_ps")
        mxT_sb = sem("mxT_sb")
        s2_ready = sem("s2_ready")
        exp_done = sem("exp_done")
        pv_done = sem("pv_done")
        o_done = sem("o_done")
        o_turned = sem("o_turned")
        inv_ready = sem("inv_ready")
        o_norm = sem("o_norm")
        oT_ps = sem("oT_ps")
        oT_ready = sem("oT_ready")
        y_ps = sem("y_ps")
        mid_ready = sem("mid_ready")
        bo_ready = sem("bo_ready")
        bvo_ps = sem("bvo_ps")
        bvo_ready = sem("bvo_ready")
        ln2 = sem("ln2")
        var2 = sem("var2")
        rstd2 = sem("rstd2")
        xn2_ready = sem("xn2_ready")
        work_set = sem("work_set")
        stage_ready = sem("stage_ready")
        xT2_ps = sem("xT2_ps")
        xT2_sb = sem("xT2_sb")
        h_ps = sem("h_ps")
        h_sb = sem("h_sb")
        out_ps = sem("out_ps")
        out_ready = sem("out_ready")
        out_stored = [sem(f"out_stored{p}") for p in range(2)]

        block = ctx.enter_context(nc.Block())

        TT = (KT + 3) // 4
        FIRST_LOADS = 16 * (PARTS + 2 * TERMS)
        UNIT_LOADS = 16 * (PARTS + 2)
        CH = cuts(KEYS)

        def chunks_ahead(half):
            def pos(n):
                return CHUNKS * (n + 2 * LEAD) // (2 * KT)
            return range(pos(half), pos(half + 1))

        def tiles(ap, n_):
            return ap[:, QT * n_:QT * (n_ + 1), :] if isinstance(n_, int) else ap[:, bass.ds(QT * n_, QT), :]

        FIRST = CHUNKS * 2 * LEAD // (2 * KT)

        @block.sync
        def _(sp):
            sp.dma_start(x_sb[:, :, :], io["x"].rearrange("b (t p) d -> p (b t) d", p=P)).then_inc(x_loaded, 16)
            for n, w in enumerate(("Wq", "Wk", "Wv")):
                sp.dma_start(w_qkv[:, n, :], io["L0_xattn_" + w]).then_inc(proj_loaded, 16)
            sp.dma_start(b_qk[:, 0:1], io["L0_xattn_bq"].rearrange("(d a) -> d a", a=1)).then_inc(proj_loaded, 16)
            sp.dma_start(b_qk[:, 1:2], io["L0_xattn_bk"].rearrange("(d a) -> d a", a=1)).then_inc(proj_loaded, 16)
            sp.dma_start(bv_col[:, :], io["L0_xattn_bv"].rearrange("(d a) -> d a", a=1)).then_inc(proj_loaded, 16)
            sp.dma_start(mask_q[:, :, :], io["mask_SxS2_fk0"].rearrange("(t p) k -> p t k", p=P)).then_inc(mask_loaded, 16)
            sp.dma_start(mask0[:, :], io["mask_SxS2_fk0"][0:1, :].to_broadcast([P, KEYS])).then_inc(mask_loaded, 16)

            def load_ctx(b, p):
                full = (KT - 1) * P
                sp.dma_start(ctx_in[:, p, 0:KT - 1, :],
                             io["ctx_1024"][b, 0:full, :].rearrange("(t p) d -> p t d", p=P)).then_inc(ctx_loaded[p], 16)
                sp.dma_start(ctx_in[0:TAIL, p, KT - 1, :], io["ctx_1024"][b, full:KEYS, :]).then_inc(ctx_loaded[p], 16)

            def leave(b, p):
                settled(sp, v_ev, TT * (b + 1) + 2)
                sp.dma_start(v_scr[b, 0:KT - 1, :, :].rearrange("t p d -> p t d"), v_out[:, p, 0:KT - 1, :]).then_inc(v_stored[p], 16)
                sp.dma_start(v_scr[b, KT - 1, 0:TAIL, :], v_out[0:TAIL, p, KT - 1, :]).then_inc(v_stored[p], 16)
                settled(sp, k_split, TT * (b + 1) + 8)
                for a in range(PARTS):
                    sp.dma_start(k_scr[b, :, a, :, :], k_pool[:, p, a, :]).then_inc(k_stored[p], 16)

            load_ctx(0, 0)
            sp.dma_start(w_o[:, :], io["L0_xattn_Wo"]).then_inc(wo_loaded, 16)
            sp.dma_start(bo_all[:, :], io["L0_xattn_bo"].rearrange("(a d) -> a d", a=1).to_broadcast([P, D])).then_inc(wo_loaded, 16)
            load_ctx(1, 1)
            sp.wait_ge(consts, 4)
            sp.wait_ge(m0_split, 1)
            for a in range(PARTS):
                sp.dma_start(ext_sb[PARTS + a:PARTS + a + 1, :], m0_parts[0:1, a * KEYS:(a + 1) * KEYS]).then_inc(ext_in, 16)
            sp.wait_ge(ctxT_ps, TT)
            load_ctx(2, 0)
            leave(0, 0)
            sp.wait_ge(ctxT_ps, 2 * TT)
            load_ctx(3, 1)
            sp.wait_ge(q_split, 3)
            for a in range(PARTS):
                sp.dma_start(q_scr[:, FIRST_TERM[a], :, :], q_bf[:, a, :]).then_inc(q_stored, 16)
            leave(1, 1)
            with sp.Fori(1, B // 2 - 1) as i:
                for p in range(2):
                    settled(sp, ctxT_ps, TT * (2 * i + p + 1))
                    load_ctx(2 * i + p + 2, p)
                    leave(2 * i + p, p)

            def first_rows(g):
                sp.dma_start(kv_k[0:XR, g, :, :], ext_sb[:, :].unsqueeze(1).to_broadcast([XR, HG, KEYS])).then_inc(ext_out[g], 16)

            def load_unit(b, g, first=False):
                h0 = HG * g
                for r0, np_ in ((0, 3), (3, 2), (5, 1)):
                    sp.dma_start(kv_k[XR + HD * r0:XR + HD * (r0 + np_), g, :, :],
                                 k_scr[b, h0:h0 + HG, 0:np_, :, :].rearrange("h a d k -> (a d) h k")).then_inc(kq_loaded[g], 16)
                if first:
                    for n in range(TERMS):
                        src = q_scr[h0:h0 + HG, FIRST_TERM[Q_PART[n]], :, 0:S].rearrange("h d s -> d h s")
                        rows = slice(XR + HD * n, XR + HD * (n + 1))
                        sp.dma_start(q1_op[rows, g, :, :], src).then_inc(kq_loaded[g], 16)
                        sp.dma_start(q2_op[rows, g, :].rearrange("r (h s) -> r h s", h=HG), src).then_inc(kq_loaded[g], 16)
                    return
                src = q_scr[h0:h0 + HG, :, :, bass.ds(b * S, S)].rearrange("h t d s -> (t d) h s")
                sp.dma_start(q1_op[XR:KR, g, :, :], src).then_inc(kq_loaded[g], 16)
                sp.dma_start(q2_op[XR:KR, g, :].rearrange("r (h s) -> r h s", h=HG), src).then_inc(kq_loaded[g], 16)

            def load_v(b):
                sp.dma_start(v_in[:, 0:KT - 1, :], v_scr[b, 0:KT - 1, :, :].rearrange("t p d -> p t d")).then_inc(v_loaded, 16)
                sp.dma_start(v_in[0:TAIL, KT - 1, :], v_scr[b, KT - 1, 0:TAIL, :]).then_inc(v_loaded, 16)

            sp.wait_ge(ext_flag, 1)
            sp.wait_ge(q_ops_set, 1)
            sp.wait_ge(slot_set, 1)
            sp.wait_ge(q_stored, 16 * PARTS)
            sp.wait_ge(k_stored[0], 48 * 2)
            first_rows(0)
            load_unit(0, 0, True)
            leave(B - 2, 0)
            leave(B - 1, 1)
            first_rows(1)
            load_unit(0, 1, True)
            load_v(0)
            for p in range(2):
                sp.wait_ge(k_stored[p], 48 * (B // 2 + 1))
                sp.wait_ge(v_stored[p], 32 * (B // 2 + 1))
            for g in range(2, G):
                sp.wait_ge(slot_set, g)
                first_rows(g)
                load_unit(0, g, True)
            for n in range(TERMS):
                if n != FIRST_TERM[Q_PART[n]]:
                    sp.dma_start(q_scr[:, n, :, :], q_scr[:, FIRST_TERM[Q_PART[n]], :, :]).then_inc(q_repeated, 16)
            sp.wait_ge(q_repeated, 16 * (TERMS - PARTS))
            sp.dma_start(wf_in.rearrange("p (c d) -> p c d", c=FC), io["L0_ffn_W_fc"].rearrange("(c p) d -> p c d", p=P)).then_inc(weights_loaded, 16)
            sp.dma_start(wp_in, io["L0_ffn_W_proj"]).then_inc(weights_loaded, 16)
            sp.dma_start(a_pj, io["L0_ffn_A_proj"]).then_inc(weights_loaded, 16)
            with sp.Fori(1, B) as i:
                for g in range(G):
                    if g == 2:
                        settled(sp, v_op_ready, G * i)
                        load_v(i)
                    settled(sp, o_done, G * i + g + 1)
                    load_unit(i, g)

            def store_out(b, p):
                sp.dma_start(io["out"][b].rearrange("(t p) d -> p t d", p=P), out_sb[:, p, :, :]).then_inc(out_stored[p], 16)

            with sp.Fori(0, B // 2) as i:
                for p in range(2):
                    settled(sp, out_ready, 2 * i + p + 1 + 1)
                    store_out(2 * i + p, p)
            for p in range(2):
                sp.wait_ge(out_stored[p], 16 * (B // 2 + 1))

        @block.gpsimd
        def _(pool):
            n = [0]

            def link(ins):
                n[0] += 1
                ins.then_inc(pool_chain, 1)
                pool.wait_ge(pool_chain, n[0])

            nc.gpsimd.memset(half_neg[:, :], -0.5)
            link(nc.gpsimd.memset(ident[:, :], 0.0))
            link(nc.gpsimd.affine_select(out=ident[:, :], in_=ident[:, :], compare_op=ALU.not_equal, fill=1.0,
                                         base=0, pattern=[[-1, P]], channel_multiplier=1))
            nc.gpsimd.tensor_copy(identb[:, :], ident[:, :]).then_inc(consts, 1)
            link(nc.gpsimd.memset(ones_m[:, :], 0.0))
            nc.gpsimd.memset(ones_m[0:PARTS, :], 1.0).then_inc(consts, 1)
            nc.gpsimd.memset(ones_f[:, :], 1.0).then_inc(consts, 1)
            nc.gpsimd.memset(ext_sb[:, :], 1.0).then_inc(consts, 1)
            nc.gpsimd.memset(x_all[:, 0:QT, :], 0.0).then_inc(work_set, 1)
            pool.wait_ge(ln_ready, 1)
            link(nc.gpsimd.tensor_scalar(ln_var[:, :], ln_var[:, :], 1.0 / D, EPS, ALU.mult, ALU.add))
            nc.gpsimd.tensor_tensor(ln_rstd[:, :], ln_var[:, :], half_neg[:, :], ALU.pow).then_inc(rstd_ready, 1)
            pool.wait_ge(tanh_ready, 1)
            link(nc.gpsimd.tensor_scalar(b_pj[:, :], b_pj[:, :], tgates[:, 1:2], None, ALU.mult))
            pool.wait_ge(mask_clamped, 2)
            nc.gpsimd.tensor_tensor(differ0, mask_q[:, 0, :], mask0[:, :], ALU.subtract).then_inc(differ_ready, 1)
            nc.gpsimd.tensor_tensor(differ1, mask_q[:, 1, :], mask0[:, :], ALU.subtract).then_inc(differ_ready, 1)
            pool.wait_ge(q_ev, 4)
            nc.gpsimd.tensor_tensor(q_full[:, :], q_full[:, :], q_bf[:, 0, :], ALU.subtract).then_inc(q_split, 1)
            pool.wait_ge(q_split, 1)
            nc.gpsimd.tensor_copy(q_bf[:, 1, :], q_full[:, :]).then_inc(q_split, 1)
            pool.wait_ge(q_split, 2)
            nc.gpsimd.tensor_tensor(q_bf[:, 2, :], q_full[:, :], q_bf[:, 1, :], ALU.subtract).then_inc(q_split, 1)
            MT = ((0, KT - 1, P), (KT - 1, KT, TAIL))

            def mT(t0, t1, rows):
                return mT_full[0:rows, t0 * S:t1 * S].rearrange("p (t s) -> p t s", s=S)

            pool.wait_ge(mT_hi, 2)
            for t0, t1, rows in MT:
                nc.gpsimd.tensor_tensor(mT(t0, t1, rows), mT(t0, t1, rows), maskT[0:rows, t0:t1, 0, :], ALU.subtract).then_inc(mT_split, 1)
            pool.wait_ge(bvo_ready, 1)
            link(nc.gpsimd.tensor_scalar(bo_all[:, :], bo_all[:, :], tgates[:, 0:1], None, ALU.mult))
            nc.gpsimd.tensor_tensor(x_sb[:, :, :], x_sb[:, :, :], bo_all[:, :].unsqueeze(1).to_broadcast([P, B * QT, D]),
                                    ALU.add).then_inc(bo_ready, 1)
            pool.wait_ge(q_stored, 16 * PARTS)
            nc.gpsimd.memset(slots[:, 0:2, :], 0.0).then_inc(slot_set, 1)
            pool.wait_ge(mT_mid, 2)
            for t0, t1, rows in MT:
                nc.gpsimd.tensor_tensor(maskT[0:rows, t0:t1, 2, :], mT(t0, t1, rows), maskT[0:rows, t0:t1, 1, :], ALU.subtract).then_inc(mT_split, 1)
            pool.wait_ge(mT_split, 4)
            link(nc.gpsimd.memset(q_ops[:, :, :].bitcast(fp32), 0.0))
            nc.gpsimd.memset(q2_op[0:XR, :, :], 1.0).then_inc(q_ops_set, 1)
            for p in range(2):
                pool.wait_ge(v_stored[p], 32 * (B // 2 + 1))
            pool.wait_ge(k_split, TT * B + 8)
            link(nc.gpsimd.memset(v_op[:, :, :, :, :], 0.0))
            nc.gpsimd.memset(v_op[:, :, :, :, HD:HD + 1], 1.0).then_inc(v_op_set, 1)
            nc.gpsimd.memset(work[:, 0:2 * S + QT * D], 1.0).then_inc(work_set, 1)
            for p in range(2):
                pool.wait_ge(k_stored[p], 48 * (B // 2 + 1))
            nc.gpsimd.memset(slots[:, 2, :], 0.0).then_inc(slot_set, 1)
            pool.wait_ge(v_op_set, 1)

            def spread_v(b, g):
                src = v_in[:, :, HD * HG * g:HD * HG * (g + 1)].rearrange("p t (h d) -> p t h d", h=HG)
                nc.gpsimd.tensor_copy(v_op[:, g, 0:KT - 1, :, 0:HD], src[:, 0:KT - 1])
                nc.gpsimd.tensor_copy(v_op[0:TAIL, g, KT - 1, :, 0:HD], src[0:TAIL, KT - 1]).then_inc(v_op_ready, 1)

            def split_max(u, par):
                settled(pool, mx_ready, u + 1)
                nc.gpsimd.tensor_copy(mx_bf[:, par, :, 0], mx_neg[:, par, :]).then_inc(mx_split, 1)
                pool.wait_ge(mx_split, 4 * u + 1)
                nc.gpsimd.tensor_tensor(mx_res[:, par, :], mx_neg[:, par, :], mx_bf[:, par, :, 0], ALU.subtract).then_inc(mx_split, 1)
                settled(pool, mx_split, 4 * u + 2)
                nc.gpsimd.tensor_copy(mx_bf[:, par, :, 1], mx_res[:, par, :]).then_inc(mx_split, 1)
                pool.wait_ge(mx_split, 4 * u + 3)
                nc.gpsimd.tensor_tensor(mx_bf[:, par, :, 2], mx_res[:, par, :], mx_bf[:, par, :, 1], ALU.subtract).then_inc(mx_split, 1)

            def rstd(n_):
                settled(pool, var2, n_ + 1)
                nc.gpsimd.tensor_scalar(l_var[:, :], l_sum[:, :], 1.0 / D, EPS, ALU.mult, ALU.add).then_inc(rstd2, 1)
                pool.wait_ge(rstd2, 2 * n_ + 1)
                nc.gpsimd.tensor_tensor(l_rstd[:, :], l_var[:, :], half_neg[:, 0:QT], ALU.pow).then_inc(rstd2, 1)
                xm = tiles(x_all, n_)
                nc.gpsimd.tensor_tensor(xm, xm, b_pj[:, :].unsqueeze(1).to_broadcast([P, QT, D]), ALU.add).then_inc(x_out, 1)

            def unit(i, g, last):
                u = G * i + g
                if g == 2:
                    rstd(i)
                if last and g == G - 1:
                    return
                nxt = G * i + g + 1
                split_max(nxt, (g + 1) % 2)
                if g == G - 1:
                    pool.wait_ge(v_loaded, 32 * (i + 2))
                settled(pool, o_done, nxt + 1)
                spread_v(i + (g + 1) // G, (g + 1) % G)

            split_max(0, 0)
            pool.wait_ge(v_loaded, 32)
            spread_v(0, 0)
            nc.gpsimd.memset(slots[:, 3, :], 0.0).then_inc(slot_set, 1)
            with pool.Fori(0, B - 1) as i:
                for g in range(G):
                    unit(i, g, False)
            for g in range(G):
                unit(B - 1, g, True)

            rstd(B)

        @block.scalar
        def _(act):
            act.dma_start(gates[:, 0:1], io["g_xattn"].rearrange("(a d) -> a d", a=1).to_broadcast([P, 1])).then_inc(ffn_loaded, 16)
            act.dma_start(gates[:, 1:2], io["g_ffn"].rearrange("(a d) -> a d", a=1).to_broadcast([P, 1])).then_inc(ffn_loaded, 16)
            act.dma_start(a_fc[:, :], io["L0_ffn_A_fc"]).then_inc(ffn_loaded, 16)
            act.dma_start(bl_fc[:, :, :], io["L0_ffn_B_fc"].rearrange("(c p) r -> p c r", p=P)).then_inc(ffn_loaded, 16)
            act.dma_start(bl_pj[:, :], io["L0_ffn_B_proj"]).then_inc(ffn_loaded, 16)
            act.dma_start(b_fc[:, :], io["L0_ffn_b_fc"].rearrange("(c p) -> p c", p=P),
                          allow_slow_non_contiguous=True).then_inc(ffn_loaded, 16)
            act.dma_start(b_pj[:, :], io["L0_ffn_b_proj"].rearrange("(a d) -> a d", a=1).to_broadcast([P, D])).then_inc(ffn_loaded, 16)
            act.wait_ge(ffn_loaded, 112)
            act.activation(tgates[:, :], gates[:, :], ACT.Tanh).then_inc(tanh_ready, 1)
            for t in range(KT):
                r = key_rows(t)
                act.wait_ge(mT_ps, t + 1)
                act.activation(mT_full[0:r, t * S:(t + 1) * S], bank(4 + t % 4)[0:r, 0:S], ACT.Copy).then_inc(mT_sb, 1)
            for c in range(4):
                act.wait_ge(xnT_ps, c + 1)
                act.activation(xnT[:, c * BANK:(c + 1) * BANK], bank(c), ACT.Copy).then_inc(xnT_sb, 1)
            act.wait_ge(proj_loaded, 96)
            nc.scalar.mul(b_qk[:, 2:3], b_qk[:, 0:1], QSCALE).then_inc(act_chain, 1)
            act.wait_ge(act_chain, 1)
            for c in range(4):
                act.wait_ge(q_ps, c + 1)
                cs = slice(c * BANK, (c + 1) * BANK)
                act.activation(q_full[:, cs], bank(4 + c), ACT.Identity, bias=b_qk[:, 2:3], scale=QSCALE)
                act.activation(q_bf[:, 0, cs], bank(4 + c), ACT.Identity, bias=b_qk[:, 2:3], scale=QSCALE).then_inc(q_ev, 1)

            act.wait_ge(ext_in, 48)
            act.wait_ge(xn_ready, 1)

            def take_ctx(b, p, c):
                m = TT * b + c
                lo, hi = CH[c]
                act.wait_ge(v_ps, m + 1)
                act.wait_ge(ctxT_ps, m + 1)
                act.activation(ctxT[:, p, lo:hi], bank(c % 2)[:, 0:hi - lo], ACT.Copy).then_inc(ctxT_sb, 1)

            def pair(i, last=False):
                for p in range(2):
                    b = 2 * i + p

                    def take_k(c):
                        m = TT * b + c
                        lo, hi = CH[c]
                        act.wait_ge(k_split, m + 1)
                        act.wait_ge(k_ps, m + 1)
                        act.activation(k_full[:, p, lo:hi], bank(2 + c % 2)[:, 0:hi - lo], ACT.Identity, bias=b_qk[:, 1:2])
                        act.activation(k_pool[:, p, 0, lo:hi], bank(2 + c % 2)[:, 0:hi - lo], ACT.Identity, bias=b_qk[:, 1:2]).then_inc(k_ev, 1)

                    def take_v(c):
                        m = TT * b + c
                        nt = min(4, KT - 4 * c)
                        rows = P if nt == 4 else TAIL
                        act.wait_ge(v_ps, m + 1 + 8)
                        act.activation(v_out[0:rows, p, 4 * c:4 * c + nt, :],
                                       bank(4 + c % 2)[0:rows, 0:nt * D].rearrange("p (t d) -> p t d", d=D), ACT.Copy).then_inc(v_ev, 1)

                    for c in range(TT):
                        if c + 1 < TT:
                            take_ctx(b, p, c + 1)
                        elif not (last and p == 1):
                            take_ctx(b + 1, 1 - p, 0)
                        if c == 0:
                            act.wait_ge(k_stored[p], 48 * (i + 1))
                            act.wait_ge(v_stored[p], 32 * (i + 1))
                        take_k(c)
                        take_v(c)

            take_ctx(0, 0, 0)
            with act.Fori(0, B // 2 - 1) as i:
                pair(i)
            pair(B // 2 - 1, last=True)

            def take_max(u, g):
                act.wait_ge(mxT_ps, u + 1)
                act.activation(q2_op[0:PARTS, g, :], bank(6 + g % 2)[:, :].bitcast(bf16)[0:PARTS, :], ACT.Copy).then_inc(mxT_sb, 1)

            def unit(i, g, last):
                for t in range(KT):
                    step = KT * (G * i + g) + t
                    r = key_rows(t)
                    slot = (KT * g + t) % 4
                    for h in range(2):
                        if h == 0:
                            act.wait_ge(pv_done, step + 1)
                        act.wait_ge(s2_ready, 2 * step + h + 1)
                        act.activation(pt[0:r, slot, h * BANK:(h + 1) * BANK], bank(4 + h)[0:r, :], ACT.Exp).then_inc(exp_done, 1)
                    if t == MX_STEP + 1 and not (last and g == G - 1):
                        take_max(G * i + g + 1, (g + 1) % G)

            take_max(0, 0)
            with act.Fori(0, B - 1) as i:
                for g in range(G):
                    unit(i, g, False)
            for g in range(G):
                unit(B - 1, g, True)

            act.wait_ge(pv_done, KT * G * B + 4)
            with act.Fori(0, B // 2) as i:
                for p in range(2):
                    for c in range(FC):
                        if c % 2 == 0:
                            act.wait_ge(h_ps, FC // 2 * (2 * i + p) + c // 2 + 1)
                        act.activation(hT[:, p, c, :], bank(2 * p + c // 2)[:, (c % 2) * S:(c % 2 + 1) * S], ACT.Gelu,
                                       bias=b_fc[:, c:c + 1]).then_inc(h_sb, 1)

        @block.vector
        def _(dve):
            n = [0]

            def link(ins):
                n[0] += 1
                ins.then_inc(dve_chain, 1)
                dve.wait_ge(dve_chain, n[0])

            for s_, d_ in ((ctxT_sb, 2), (k_ev, 2), (v_ps, 8), (v_ev, 2), (k_split, 8), (pv_done, 4), (o_done, 4),
                           (k_stored[0], 48), (k_stored[1], 48), (v_stored[0], 32), (v_stored[1], 32), (out_stored[0], 16), (out_stored[1], 16),
                           (o_norm, 1), (out_ready, 1)):
                dve.sem_inc(s_, d_)
            def bc(ap):
                return ap.unsqueeze(2).to_broadcast([P, B * QT, D])
            dve.wait_ge(x_loaded, 16)
            link(nc.vector.reduce_sum(ln_sum[:, :], x_sb[:, :, :], AX.X))
            link(nc.vector.tensor_scalar(ln_mean[:, :], ln_sum[:, :], 1.0 / D, None, ALU.mult))
            link(nc.vector.tensor_tensor(qn[:, :, :], x_sb[:, :, :], bc(ln_mean[:, :]), ALU.subtract))
            link(nc.vector.tensor_tensor(qsq[:, :, :], qn[:, :, :], qn[:, :, :], ALU.mult))
            nc.vector.reduce_sum(ln_var[:, :], qsq[:, :, :], AX.X).then_inc(ln_ready, 1)
            dve.wait_ge(mask_loaded, 32)
            nc.vector.tensor_scalar(mask_q[:, :, :], mask_q[:, :, :], -BIG, BIG, ALU.max, ALU.min).then_inc(mask_clamped, 1)
            dve.wait_ge(rstd_ready, 1)
            nc.vector.tensor_tensor(qn[:, :, :], qn[:, :, :], bc(ln_rstd[:, :]), ALU.mult).then_inc(xn_ready, 1)
            nc.vector.tensor_scalar(mask0[:, :], mask0[:, :], -BIG, BIG, ALU.max, ALU.min).then_inc(mask_clamped, 1)
            dve.wait_ge(mask_clamped, 2)
            link(nc.vector.tensor_copy(m0_parts[0:1, 0:KEYS], mask0[0:1, :]))
            link(nc.vector.tensor_tensor(m0_res[0:1, :], mask0[0:1, :], m0_parts[0:1, 0:KEYS], ALU.subtract))
            link(nc.vector.tensor_copy(m0_parts[0:1, KEYS:2 * KEYS], m0_res[0:1, :]))
            nc.vector.tensor_tensor(m0_parts[0:1, 2 * KEYS:3 * KEYS], m0_res[0:1, :], m0_parts[0:1, KEYS:2 * KEYS], ALU.subtract).then_inc(m0_split, 1)
            link(nc.vector.reduce_max(rng[:, 2:3], mask0[:, :], AX.X))
            link(nc.vector.tensor_scalar(rng[:, 3:4], rng[:, 2:3], PLAIN_TOP, None, ALU.is_gt))
            link(nc.vector.tensor_scalar(rng[:, 2:3], rng[:, 2:3], -PLAIN_TOP, None, ALU.is_lt))
            dve.wait_ge(mT_sb, KT)
            for t0, t1, rows in ((0, KT - 1, P), (KT - 1, KT, TAIL)):
                nc.vector.tensor_copy(maskT[0:rows, t0:t1, 0, :],
                                      mT_full[0:rows, t0 * S:t1 * S].rearrange("p (t s) -> p t s", s=S)).then_inc(mT_hi, 1)

            dve.wait_ge(differ_ready, 2)
            nc.vector.tensor_reduce(rng[:, 0:1], differ0, AX.X, ALU.max, apply_absolute_value=True)
            link(nc.vector.tensor_reduce(rng[:, 1:2], differ1, AX.X, ALU.max, apply_absolute_value=True))
            link(nc.vector.tensor_scalar(rng[:, 0:2], rng[:, 0:2], 0.0, None, ALU.is_gt))
            nc.vector.tensor_reduce(stat_m[:, :], rng[:, :], AX.X, ALU.max).then_inc(flag_part, 1)
            dve.wait_ge(bvo_ps, 1)
            nc.vector.tensor_tensor(bo_all[:, :], bank(6)[:, 0:D], bo_all[:, :], ALU.add).then_inc(bvo_ready, 1)

            ksub = sem("ksub")
            dve.wait_ge(ext_in, 48)

            def pair(i):
                for p in range(2):
                    b = 2 * i + p
                    for c in range(TT):
                        m = TT * b + c
                        lo, hi = CH[c]
                        if c == 0:
                            dve.wait_ge(k_stored[p], 48 * (i + 1))
                        dve.wait_ge(k_ev, m + 1 + 2)
                        nc.vector.tensor_tensor(k_res[:, lo:hi], k_full[:, p, lo:hi], k_pool[:, p, 0, lo:hi], ALU.subtract).then_inc(ksub, 1)
                        dve.wait_ge(ksub, 2 * m + 1)
                        nc.vector.tensor_copy(k_pool[:, p, 1, lo:hi], k_res[:, lo:hi]).then_inc(ksub, 1)
                        dve.wait_ge(ksub, 2 * m + 2)
                        nc.vector.tensor_tensor(k_pool[:, p, 2, lo:hi], k_res[:, lo:hi], k_pool[:, p, 1, lo:hi], ALU.subtract).then_inc(k_split, 1)

            pair(0)
            dve.wait_ge(flag_ps, 1)
            nc.vector.reduce_max(flag_t[:, :], bank(6)[0:1, 0:P], AX.X).then_inc(flag_row, 1)
            dve.wait_ge(flag_row, 1)
            nc.vector.tensor_copy(general_i[:, :], flag_t[:, :]).then_inc(flag_ready, 1)
            pair(1)
            dve.wait_ge(flag_ps, 2)
            link(nc.vector.tensor_scalar(plain[:, :], bank(6)[:, 0:1], -1.0, 1.0, ALU.mult, ALU.add))
            nc.vector.tensor_scalar(ext_sb[:, :], ext_sb[:, :], plain[0:XR, 0:1], None, ALU.mult).then_inc(ext_flag, 1)
            dve.wait_ge(mT_split, 2)
            for t0, t1, rows in ((0, KT - 1, P), (KT - 1, KT, TAIL)):
                nc.vector.tensor_copy(maskT[0:rows, t0:t1, 1, :],
                                      mT_full[0:rows, t0 * S:t1 * S].rearrange("p (t s) -> p t s", s=S)).then_inc(mT_mid, 1)
            with dve.Fori(2, B // 2) as i:
                pair(i)

            def chunk(i, g, c):
                u = G * i + g
                qh, half = c // 2, c % 2
                lo = half * HALF
                width = min(HALF, KEYS - lo)
                pos = CHUNKS * u + c
                two = ps[:, 2 * half:2 * half + 2, :].rearrange("p a n -> p (a n)")
                settled(dve, s1_ready, pos + 1)
                nc.vector.tensor_tensor_reduce(out=two[:, 0:width], in0=two[:, 0:width],
                                               in1=mask_q[:, qh % QT, lo:lo + width], scale=1.0, scalar=-3.4e38,
                                               op0=ALU.add, op1=ALU.max,
                                               accum_out=mx_part[:, g % 2, qh, half:half + 1]).then_inc(s1_done, 1)
                if c == CHUNKS - 1:
                    dve.wait_ge(s1_done, pos + 1)
                    nc.vector.tensor_reduce(mx_neg[:, g % 2, :], mx_part[:, g % 2, :, :], AX.X, ALU.max,
                                            negate=True).then_inc(mx_ready, 1)

            def normalise(u, slot):
                turned = bank(6 + slot % 2)[:, S:2 * S].rearrange("p (t j r) -> p t j r", t=QT, j=HG)
                dve.wait_ge(o_norm, u + 1)
                settled(dve, o_turned, u + 1)
                nc.vector.reciprocal(o_inv[:, :, :], turned[:, :, :, HD]).then_inc(inv_ready, 1)
                dve.wait_ge(inv_ready, u + 1)
                nc.vector.tensor_tensor(o_q[:, :, HG * HD * slot:HG * HD * (slot + 1)].rearrange("p t (j d) -> p t j d", j=HG),
                                        turned[:, :, :, 0:HD], o_inv[:, :, :].unsqueeze(3).to_broadcast([P, QT, HG, HD]),
                                        ALU.mult).then_inc(o_norm, 1)

            def take_oT(n_):
                dve.wait_ge(oT_ps, n_ + 1)
                nc.vector.tensor_copy(oT, bank(7)[:, 0:S]).then_inc(oT_ready, 1)

            def take_y(n_):
                dve.wait_ge(y_ps, n_ + 1)
                nc.vector.scalar_tensor_tensor(out=tiles(x_all, n_), in0=bank(7)[:, S:S + QT * D].rearrange("p (t d) -> p t d", t=QT),
                                               scalar=tgates[:, 0:1], in1=tiles(x_all, n_),
                                               op0=ALU.mult, op1=ALU.add).then_inc(mid_ready, 1)

            def norm_step(n_, k):
                xm = tiles(x_all, n_)
                if k == 0:
                    settled(dve, mid_ready, n_ + 1)
                    nc.vector.reduce_sum(l_mean[:, :], xm, AX.X).then_inc(ln2, 1)
                elif k == 1:
                    dve.wait_ge(ln2, 4 * n_ + 1)
                    nc.vector.tensor_scalar(l_mean[:, :], l_mean[:, :], 1.0 / D, None, ALU.mult).then_inc(ln2, 1)
                elif k == 2:
                    dve.wait_ge(ln2, 4 * n_ + 2)
                    nc.vector.tensor_tensor(x_c, xm, l_mean[:, :].unsqueeze(2).to_broadcast([P, QT, D]), ALU.subtract).then_inc(ln2, 1)
                elif k == 3:
                    dve.wait_ge(ln2, 4 * n_ + 3)
                    nc.vector.tensor_tensor(x_q, x_c, x_c, ALU.mult).then_inc(ln2, 1)
                elif k == 4:
                    dve.wait_ge(ln2, 4 * n_ + 4)
                    nc.vector.reduce_sum(l_sum[:, :], x_q, AX.X).then_inc(var2, 1)
                else:
                    dve.wait_ge(rstd2, 2 * n_ + 2)
                    nc.vector.tensor_tensor(tiles(x_n, n_), x_c, l_rstd[:, :].unsqueeze(2).to_broadcast([P, QT, D]),
                                            ALU.mult).then_inc(xn2_ready, 1)

            def stage(b, p=None):
                p = b % 2 if p is None else p
                settled(dve, xn2_ready, b + 2)
                nc.vector.tensor_copy(x_nS[:, p, :, :], tiles(x_n, b + 1)).then_inc(stage_ready, 1)

            def take_x(b, p=None):
                p = b % 2 if p is None else p
                dve.wait_ge(xT2_ps, b + 1)
                nc.vector.tensor_copy(x_nT[:, p, :], bank(6)[:, 0:S]).then_inc(xT2_sb, 1)

            def finish(b, p=None, i=0):
                p = b % 2 if p is None else p
                i = b // 2 if isinstance(b, int) else i
                dve.wait_ge(out_stored[p], 16 * (i + 1))
                dve.wait_ge(x_out, b + 2)
                dve.wait_ge(out_ps, b + 1)
                nc.vector.scalar_tensor_tensor(out=out_sb[:, p, :, :], in0=bank(4 + p)[:, 0:QT * D].rearrange("p (t d) -> p t d", t=QT),
                                               scalar=tgates[:, 1:2], in1=tiles(x_all, b + 1),
                                               op0=ALU.mult, op1=ALU.add).then_inc(out_ready, 1)

            def quantise(k, w, r_):
                link(nc.vector.tensor_scalar(wf_a, w, inv_s[:, 2 + k:3 + k], MAGIC, ALU.mult, ALU.add))
                link(nc.vector.tensor_scalar(wf_b, wf_a, -MAGIC, -QMAX - 1.0, ALU.add, ALU.max))
                link(nc.vector.tensor_scalar(wf_a, wf_b, QMAX, inv_s[:, k:k + 1], ALU.min, ALU.mult))
                link(nc.vector.tensor_tensor(wf_b, wf_a, w, ALU.subtract))
                nc.vector.tensor_tensor(r_, wf_b, w, ALU.add).then_inc(wq_ready, 1)
                dve.wait_ge(wq_ready, 1 + k)

            def prepare(t):
                if t == PREPARE:
                    dve.wait_ge(weights_loaded, 48)
                    link(nc.vector.tensor_reduce(stat[:, 0:1], wf_in, AX.X, ALU.max, apply_absolute_value=True))
                    nc.vector.tensor_reduce(stat[:, 1:2], wp_in, AX.X, ALU.max, apply_absolute_value=True).then_inc(stat_ready, 1)
                if t == PREPARE + 1:
                    dve.wait_ge(lora_ps, 1)
                    nc.vector.tensor_scalar(blT_fc, bank(0)[0:RANK, :], 2.0, None, ALU.mult).then_inc(lora_sb, 1)
                    dve.wait_ge(lora_ps, 2)
                    nc.vector.tensor_scalar(blT_pj[:, :], bank(1)[0:RANK, 0:D], 2.0, None, ALU.mult).then_inc(lora_sb, 1)
                    dve.wait_ge(stat_ps, 1)
                    link(nc.vector.reduce_max(stat_t[:, :], bank(2)[0:2, 0:P], AX.X))
                    nc.vector.tensor_scalar(stat_d[:, :], ident[0:2, 0:2], stat_t[:, 0:1], None, ALU.mult).then_inc(stat_diag, 1)
                if t == PREPARE + 2:
                    dve.wait_ge(stat_ps, 2)
                    link(nc.vector.tensor_copy(allstat[:, :], bank(2)[:, 0:2]))
                    link(nc.vector.tensor_scalar(inv_s[:, 0:2], allstat[:, :], 1.0 / QMAX, None, ALU.mult))
                    link(nc.vector.reciprocal(inv_s[:, 2:4], inv_s[:, 0:2]))
                    quantise(0, wf_in, wf_r)
                if t == KT + O_STEP + 2:
                    quantise(1, wp_in, wp_r)
                    stage(0)
                    stage(1)
                if t == 2 * KT - 4:
                    dve.wait_ge(weff_ps, 1)
                    nc.vector.tensor_copy(w_fcT[:, :], bank(0)).then_inc(weff_sb, 1)
                    dve.wait_ge(weff_ps, 2)
                    nc.vector.tensor_copy(w_pjT[:, :, :].rearrange("p c d -> p (c d)"), bank(1)).then_inc(weff_sb, 1)
                    take_x(0)
                    stage(2)
                    take_x(1)

            def unit(i, g, last):
                u = G * i + g
                for t in range(KT):
                    for c in [*chunks_ahead(2 * t), *chunks_ahead(2 * t + 1)]:
                        ahead = g + 1 + c // CHUNKS
                        if not (last and ahead >= G):
                            chunk(i, ahead, c % CHUNKS)
                    if t == O_STEP + 1:
                        normalise(u, (g - 1) % G)
                    if g == 0 and t == OT_STEP + 1:
                        take_oT(i)
                    if g == 0 and t == Y_STEP + 1:
                        take_y(i)
                    if (g, t) in LN_STEPS:
                        norm_step(i, LN_STEPS.index((g, t)))
                    if last and g >= G - 2:
                        prepare(KT * (g - G + 2) + t)
                dve.wait_ge(pv_done, KT * (u + 1) + 4)
                nc.vector.tensor_copy(o_raw[:, g % 2, :], bank(6 + g % 2)[:, 0:S]).then_inc(o_done, 1)

            for c in range(CHUNKS):
                chunk(0, 0, c)
            for c in range(FIRST):
                chunk(0, 1, c)
            with dve.Fori(0, B - 1) as i:
                for g in range(G):
                    unit(i, g, False)
            for g in range(G):
                unit(B - 1, g, True)

            normalise(B * G, G - 1)
            take_oT(B)
            take_x(2)
            take_y(B)
            for k in range(5):
                norm_step(B, k)
            stage(3)
            finish(0)
            norm_step(B, 5)
            with dve.Fori(0, B // 2 - 2) as i:
                for k in (1, 2):
                    b = 2 * i + k
                    take_x(b + 2, k % 2)
                    stage(b + 3, 1 - k % 2)
                    finish(b, k % 2, i + k // 2)
            take_x(B - 1)
            for b in (B - 3, B - 2, B - 1):
                finish(b)

        @block.tensor
        def _(pe):
            pe.wait_ge(consts, 4)
            pe.wait_ge(mask_clamped, 1)
            for t in range(KT):
                r = key_rows(t)
                if t >= 4:
                    pe.wait_ge(mT_sb, t - 3)
                for k in range(QT):
                    m = nc.tensor.transpose(bank(4 + t % 4)[0:r, k * P:(k + 1) * P], mask_q[:, k, t * P:t * P + r], ident[:, :])
                m.then_inc(mT_ps, 1)
            pe.wait_ge(xn_ready, 1)
            for c in range(4):
                for k in range(4):
                    m = nc.tensor.transpose(bank(c)[:, k * P:(k + 1) * P], qn[:, 4 * c + k, :], ident[:, :])
                m.then_inc(xnT_ps, 1)
            pe.wait_ge(proj_loaded, 96)
            pe.wait_ge(mT_sb, KT)
            for c in range(4):
                pe.wait_ge(xnT_sb, c + 1)
                nc.tensor.matmul(bank(4 + c), w_qkv[:, 0, :], xnT[:, c * BANK:(c + 1) * BANK], start=True, stop=True).then_inc(q_ps, 1)
            pe.wait_ge(q_ev, 3)
            pe.wait_ge(wo_loaded, 32)
            nc.tensor.matmul(bank(6)[:, 0:D], bv_col[:, 0:1].to_broadcast([P, P]), w_o[:, :], start=True, stop=True).then_inc(bvo_ps, 1)

            def turn(b, p, i, c):
                if c == 0:
                    pe.wait_ge(ctx_loaded[p], 32 * (i + 1))
                pe.wait_ge(ctxT_sb, TT * b + c + 1)
                for t in range(4 * c, min(4 * c + 4, KT)):
                    r = key_rows(t)
                    m = nc.tensor.transpose(bank(c % 2)[:, (t % 4) * P:(t % 4) * P + r], ctx_in[0:r, p, t, :], ident[0:r, 0:r])
                m.then_inc(ctxT_ps, 1)

            def pair(i, last=False):
                for p in range(2):
                    b = 2 * i + p

                    def project(c):
                        n_ = TT * b + c
                        lo, hi = CH[c]
                        pe.wait_ge(ctxT_sb, n_ + 1 + 2)
                        pe.wait_ge(k_ev, n_ + 1)
                        nc.tensor.matmul(bank(2 + c % 2)[:, 0:hi - lo], w_qkv[:, 1, :], ctxT[:, p, lo:hi],
                                         start=True, stop=True).then_inc(k_ps, 1)
                        pe.wait_ge(v_ev, n_ + 1)
                        for t in range(4 * c, min(4 * c + 4, KT)):
                            r = key_rows(t)
                            m = nc.tensor.matmul(bank(4 + c % 2)[0:r, (t % 4) * D:(t % 4 + 1) * D],
                                                 ctxT[:, p, t * P:t * P + r], w_qkv[:, 2, :], start=True, stop=True)
                        m.then_inc(v_ps, 1)

                    for c in range(TT):
                        if c + 1 < TT:
                            turn(b, p, i, c + 1)
                        elif not (last and p == 1):
                            turn(b + 1, 1 - p, i + p, 0)
                        if isinstance(i, int) and i == 0 and p == 0 and c == 0:
                            pe.wait_ge(q_ev, 4)
                        project(c)

            turn(0, 0, 0, 0)
            pair(0)
            pe.wait_ge(flag_part, 1)
            pe.wait_ge(bvo_ready, 1)
            nc.tensor.transpose(bank(6)[0:1, 0:P], stat_m[:, :], ident[:, :]).then_inc(flag_ps, 1)
            pair(1)
            pe.wait_ge(flag_row, 1)
            nc.tensor.matmul(bank(6)[:, 0:1], ones_f[0:1, :], flag_t[:, :], start=True, stop=True).then_inc(flag_ps, 1)
            with pe.Fori(2, B // 2 - 1) as i:
                pair(i)
            pair(B // 2 - 1, last=True)
            pe.wait_ge(flag_ready, 1)
            pe.wait_ge(ext_flag, 1)
            general = pe.value_load(general_i[0:1, 0:1], min_val=0, max_val=1)

            def chunk(i, g, c):
                u = G * i + g
                slot = g % G
                qh, half = c // 2, c % 2
                h, qt = qh // QT, qh % QT
                lo = half * HALF
                width = min(HALF, KEYS - lo)
                pos = CHUNKS * u + c
                if c == 0:
                    pe.wait_ge(kq_loaded[slot], FIRST_LOADS + UNIT_LOADS * (i + g // G))
                    pe.wait_ge(ext_out[slot], 16)
                if not (isinstance(i, int) and pos < 2):
                    pe.wait_ge(s1_done, pos - 1)
                for k, (a, z) in enumerate(cuts(width)):
                    m = nc.tensor.matmul(ps[:, 2 * half + k, 0:z - a], q1_op[:, slot, h, qt * P:(qt + 1) * P],
                                         kv_k[:, slot, h, lo + a:lo + z], start=True, stop=True)
                m.then_inc(s1_ready, 1)

            def turn_max(u, slot, batch):
                pe.wait_ge(mx_split, 4 * (u + 1))
                pe.wait_ge(o_norm, u + 1)
                if slot == 1:
                    pe.wait_ge(mid_ready, batch + 1)
                rows = bank(6 + slot % 2)[:, :].bitcast(bf16)
                for j in range(HG * QT):
                    m = nc.tensor.transpose(rows[0:PARTS, j * P:(j + 1) * P], mx_bf[:, slot % 2, j, :], identb[:, :])
                m.then_inc(mxT_ps, 1)

            def sweep2(i, g, t, arm):
                slot = g % G
                step = KT * (G * i + g) + t
                r = key_rows(t)
                if t == 0:
                    pe.wait_ge(mxT_sb, G * i + g + 1)
                for k in range(2):
                    if not (isinstance(i, int) and step == 0):
                        pe.wait_ge(exp_done, 2 * step + k - 1)
                    out = bank(4 + k)[0:r, :]
                    if arm == "general":
                        for a in range(PARTS):
                            nc.tensor.matmul(out.rearrange("p (h s) -> p h s", h=2), identb[0:r, 0:r],
                                             maskT[0:r, t, a, :].unsqueeze(1).to_broadcast([r, 2, S]),
                                             start=(a == 0), stop=False)
                    for h in range(2 * k, 2 * k + 2):
                        m = nc.tensor.matmul(out[:, (h % 2) * S:(h % 2 + 1) * S], kv_k[:, slot, h, t * P:t * P + r],
                                             q2_op[:, slot, h * S:(h + 1) * S],
                                             start=(arm != "general"), stop=(arm != "general"))
                    if arm == "general":
                        m = nc.tensor.matmul(out, ones_m[:, 0:r], q2_op[:, slot, 2 * k * S:(2 * k + 2) * S],
                                             start=False, stop=True)
                    m.then_inc(s2_ready, 1)

            def multiply_v(i, g, t):
                step = KT * (G * i + g) + t
                r = key_rows(t)
                if t == 0:
                    pe.wait_ge(v_op_ready, G * i + g + 1)
                pe.wait_ge(exp_done, 2 * step + 2)
                for h in range(HG):
                    m = nc.tensor.matmul(bank(6 + g % 2)[32 * h:32 * h + 32, 0:S], v_op[0:r, g, t, h, :],
                                         pt[0:r, (KT * g + t) % 4, h * S:(h + 1) * S],
                                         start=(t == 0), stop=(t == KT - 1))
                m.then_inc(pv_done, 1)

            def turn_o(u, par):
                pe.wait_ge(o_done, u + 4)
                for t in range(QT):
                    m = nc.tensor.transpose(bank(6 + par)[:, S + t * P:S + (t + 1) * P], o_raw[:, par, t * P:(t + 1) * P], ident[:, :])
                m.then_inc(o_turned, 1)

            def turn_back(n_):
                pe.wait_ge(o_norm, G * n_ + 1 + 1)
                for t in range(QT):
                    m = nc.tensor.transpose(bank(7)[:, t * P:(t + 1) * P], o_q[:, t, :], ident[:, :])
                m.then_inc(oT_ps, 1)

            def project_o(n_):
                pe.wait_ge(oT_ready, n_ + 1)
                for t in range(QT):
                    m = nc.tensor.matmul(bank(7)[:, S + t * D:S + (t + 1) * D], oT[:, t * P:(t + 1) * P], w_o[:, :],
                                         start=True, stop=True)
                m.then_inc(y_ps, 1)

            def turn_x(b, p=None):
                p = b % 2 if p is None else p
                pe.wait_ge(stage_ready, b + 1)
                if not (isinstance(b, int) and b == 0):
                    pe.wait_ge(xT2_sb, b)
                for t in range(QT):
                    m = nc.tensor.transpose(bank(6)[:, t * P:(t + 1) * P], x_nS[:, p, t, :], ident[:, :])
                m.then_inc(xT2_ps, 1)

            def widen(b, p=None):
                p = b % 2 if p is None else p
                pe.wait_ge(xT2_sb, b + 1)
                for c in range(FC):
                    m = nc.tensor.matmul(bank(2 * p + c // 2)[:, (c % 2) * S:(c % 2 + 1) * S], w_fcT[:, c * P:(c + 1) * P],
                                         x_nT[:, p, :], start=True, stop=True)
                    if c % 2:
                        m.then_inc(h_ps, 1)

            def narrow(b, p=None):
                p = b % 2 if p is None else p
                if not (isinstance(b, int) and b == 0):
                    pe.wait_ge(out_ready, b)
                for t in range(QT):
                    for c in range(FC):
                        if t == 0:
                            pe.wait_ge(h_sb, FC * b + c + 1)
                        m = nc.tensor.matmul(bank(4 + p)[:, t * D:(t + 1) * D], hT[:, p, c, t * P:(t + 1) * P], w_pjT[:, c, :],
                                             start=(c == 0), stop=(c == FC - 1))
                m.then_inc(out_ps, 1)

            def prepare(t):
                if t == PREPARE + 1:
                    pe.wait_ge(s1_done, CHUNKS * G * B)
                    pe.wait_ge(ffn_loaded, 112)
                    for c in range(FC):
                        m = nc.tensor.transpose(bank(0)[0:RANK, c * P:(c + 1) * P], bl_fc[:, c, :], ident[:, :])
                    m.then_inc(lora_ps, 1)
                    nc.tensor.transpose(bank(1)[0:RANK, 0:P], bl_pj[:, :], ident[:, :]).then_inc(lora_ps, 1)
                    pe.wait_ge(stat_ready, 1)
                    nc.tensor.transpose(bank(2)[0:2, 0:P], stat[:, :], ident[:, :]).then_inc(stat_ps, 1)
                if t == PREPARE + 2:
                    pe.wait_ge(stat_diag, 1)
                    nc.tensor.matmul(bank(2)[:, 0:2], ones_f[0:2, :], stat_d[:, :], start=True, stop=True).then_inc(stat_ps, 1)
                if t == KT + 3:
                    pe.wait_ge(lora_sb, 2)
                    pe.wait_ge(wq_ready, 1)
                    for c in range(FC):
                        cs = slice(c * P, (c + 1) * P)
                        nc.tensor.matmul(bank(0)[:, cs], wf_r[:, cs], ident[:, :], start=True, stop=False)
                        m = nc.tensor.matmul(bank(0)[:, cs], a_fc[:, :], blT_fc[:, cs], start=False, stop=True)
                    m.then_inc(weff_ps, 1)
                if t == KT + 8:
                    pe.wait_ge(wq_ready, 2)
                    for c in range(FC):
                        cs = slice(c * P, (c + 1) * P)
                        nc.tensor.matmul(bank(1)[:, cs], wp_r[:, cs], ident[:, :], start=True, stop=False)
                        m = nc.tensor.matmul(bank(1)[:, cs], a_pj[:, cs], blT_pj[:, :], start=False, stop=True)
                    m.then_inc(weff_ps, 1)
                if t == KT + 9:
                    pe.wait_ge(o_norm, G * B + 1)
                    turn_x(0)
                if t == KT + 11:
                    turn_x(1)
                if t == KT + 12:
                    pe.wait_ge(weff_sb, 2)
                    widen(0)

            def unit(i, g, last, arm):
                final = last and g == G - 1

                def ahead(half):
                    for c in chunks_ahead(half):
                        unit_ = g + 1 + c // CHUNKS
                        if not (last and unit_ >= G):
                            chunk(i, unit_, c % CHUNKS)

                for t in range(KT):
                    ahead(2 * t)
                    if t + 1 < KT:
                        sweep2(i, g, t + 1, arm)
                    elif not final:
                        sweep2(i, g + 1, 0, arm)
                    if t == O_STEP:
                        turn_o(G * i + g, (g - 1) % 2)
                    if g == 0 and t == OT_STEP:
                        turn_back(i)
                    if g == 0 and t == Y_STEP:
                        project_o(i)
                    if t == MX_STEP and not final:
                        turn_max(G * i + g + 1, (g + 1) % G, i)
                    ahead(2 * t + 1)
                    if last and g >= G - 2:
                        prepare(KT * (g - G + 2) + t)
                    multiply_v(i, g, t)

            def either(body):
                with pe.If(general != 0):
                    body("general")
                with pe.Else():
                    body("plain")

            pe.wait_ge(wo_loaded, 32)
            pe.wait_ge(mT_split, 4)
            for left in (ctxT_sb, k_ev, v_ev):
                pe.wait_ge(left, TT * B + 2)
            for c in range(CHUNKS):
                chunk(0, 0, c)
            for c in range(FIRST):
                chunk(0, 1, c)
                if c == 2:
                    turn_max(0, 0, 0)
            pe.wait_ge(work_set, 2)
            either(lambda arm: sweep2(0, 0, 0, arm))
            with pe.Fori(0, B - 1) as i:
                either(lambda arm: [unit(i, g, False, arm) for g in range(G)])
            either(lambda arm: [unit(B - 1, g, True, arm) for g in range(G)])

            turn_o(B * G, 1)
            widen(1)
            turn_back(B)
            turn_x(2)
            narrow(0)
            project_o(B)
            widen(2)
            with pe.Fori(0, B // 2 - 2) as i:
                for k in (1, 2):
                    b = 2 * i + k
                    turn_x(b + 2, k % 2)
                    narrow(b, k % 2)
                    widen(b + 2, k % 2)
            turn_x(B - 1)
            narrow(B - 3)
            widen(B - 1)
            narrow(B - 2)
            narrow(B - 1)

_INS = ['x', 'ctx_1024', 'mask_SxS2_fk0', 'g_xattn', 'g_ffn', 'L0_xattn_Wq', 'L0_xattn_bq', 'L0_xattn_Wk', 'L0_xattn_bk',
        'L0_xattn_Wv', 'L0_xattn_bv', 'L0_xattn_Wo', 'L0_xattn_bo', 'L0_ffn_W_fc', 'L0_ffn_b_fc', 'L0_ffn_A_fc',
        'L0_ffn_B_fc', 'L0_ffn_W_proj', 'L0_ffn_b_proj', 'L0_ffn_A_proj', 'L0_ffn_B_proj']


def kernel(**inputs):
    import numpy as _np
    import concourse.bacc as _bacc
    from concourse import mybir as _mybir
    from concourse.bass_utils import run_bass_kernel_spmd as _run

    nc = _bacc.Bacc("TRN2", target_bir_lowering=False, num_devices=1)
    arrays, io = {}, {}
    for name in _INS:
        a = _np.ascontiguousarray(inputs[name])
        arrays[f"in_{name}"] = a
        io[name] = nc.dram_tensor(f"in_{name}", a.shape, _mybir.dt.from_np(a.dtype), kind="ExternalInput").ap()
    shape = arrays["in_x"].shape
    io["out"] = nc.dram_tensor("out_0", shape, _mybir.dt.float32, kind="ExternalOutput").ap()
    flamingo_block(nc, io)
    r = _run(nc, [arrays], core_ids=[0])
    return r.results[0]["out_0"]
```
